# Optimizing a Trainium2 kernel written in Bass

```python
import numpy as np
import jax
import jax.numpy as jnp

def _softmax(x, axis=-1):
    return jax.nn.softmax(x, axis=axis)
def _gelu(x):
    return jax.nn.gelu(x, approximate=True)
def _silu(x):
    return jax.nn.silu(x)
def _sigmoid(x):
    return jax.nn.sigmoid(x)
def _layernorm(x, axis=-1, eps=1e-5):
    m = jnp.mean(x, axis=axis, keepdims=True)
    v = jnp.var(x, axis=axis, keepdims=True)
    return (x - m) / jnp.sqrt(v + eps)
def _scatter_add(tgt, idx, src, axis=0):
    return tgt.at[idx].add(src)
def _segment_sum(src, seg, n):
    return jax.ops.segment_sum(src, seg, n)

kernel_name = 'mk_conv_preact_d2_conv_nchw384_34d6cf'

def setup_inputs(seed: int = 0):
    np.random.seed(seed)
    _w = jnp.asarray
    def _rec_inputs():
        import jax
        import jax.numpy as jnp
        _gk = jax.random.key(seed)
        x = -0.0004039 + 1 * jax.random.normal(jax.random.fold_in(_gk, 1), (8, 384, 64, 64), jnp.float32)
        return x
    x = _rec_inputs()
    def _L0_conv_setup():
        import jax, jax.numpy as jnp
        import numpy as np
        THETA = 10000.0
        EMBED_DIM = 384
        NUM_HEADS = 6

        def apply_rope_2d(x):
            B, C, H, W = x.shape
            dim = C // 2
            inv = 1.0 / THETA ** (jnp.arange(0, dim, 2, dtype=x.dtype) / dim)
            fh = jnp.arange(H, dtype=x.dtype)[:, None] * inv[None, :]
            fw = jnp.arange(W, dtype=x.dtype)[:, None] * inv[None, :]
            fh_flat = jnp.broadcast_to(fh[:, None, :], (H, W, dim // 2)).reshape(H * W, dim // 2)
            fw_flat = jnp.broadcast_to(fw[None, :, :], (H, W, dim // 2)).reshape(H * W, dim // 2)
            x_seq = x.reshape(B, C, H * W).transpose(0, 2, 1)
            x_h, x_w = (x_seq[..., :dim], x_seq[..., dim:])

            def apply_rotary(t, f):
                cos = jnp.repeat(jnp.cos(f), 2, axis=-1)
                sin = jnp.repeat(jnp.sin(f), 2, axis=-1)
                t1, t2 = jnp.split(t, 2, axis=-1)
                rot = jnp.concatenate([-t2, t1], axis=-1)
                return t * cos + rot * sin
            x_h = apply_rotary(x_h, fh_flat)
            x_w = apply_rotary(x_w, fw_flat)
            x_out = jnp.concatenate([x_h, x_w], axis=-1)
            return x_out.transpose(0, 2, 1).reshape(B, C, H, W)

        def conv1x1(x, W, b):
            return jnp.einsum('oc,bchw->bohw', W, x) + b[None, :, None, None]
        key = jax.random.key(seed)
        ks = jax.random.split(key, 9)
        B, C, H, W = (8, EMBED_DIM, 64, 64)
        s = 1.0 / np.sqrt(C)
        inp = {'x': jax.random.normal(ks[0], (B, C, H, W), dtype=jnp.float32)}
        for i, name in enumerate(['q', 'k', 'v', 'fc']):
            inp[f'W{name}'] = jax.random.uniform(ks[1 + 2 * i], (C, C), dtype=jnp.float32, minval=-s, maxval=s)
            inp[f'b{name}'] = jax.random.uniform(ks[2 + 2 * i], (C,), dtype=jnp.float32, minval=-s, maxval=s)
        return inp
    _L0_conv_all = _L0_conv_setup()
    _L0_conv_in = {k: v for k, v in _L0_conv_all.items() if k in ('Wq', 'bq', 'Wk', 'bk', 'Wv', 'bv', 'Wfc', 'bfc', )}
    del _L0_conv_all

    def _L1_conv_setup():
        import jax, jax.numpy as jnp
        import numpy as np
        B, DIM, H, W = (2, 384, 256, 256)
        HID = DIM * 1
        P = 8
        key = jax.random.key(seed)
        k0, k1, k2, k3, k4 = jax.random.split(key, 5)
        x = jax.random.normal(k0, (B, DIM, H, W), jnp.float32)
        fft_filter = jax.random.normal(k1, (HID, P, P // 2 + 1), jnp.float32)
        w_in = jax.random.normal(k2, (HID, DIM), jnp.float32) * (1.0 / np.sqrt(DIM))
        w_dw = jax.random.normal(k3, (HID, 1, 3, 3), jnp.float32) * (1.0 / 3.0)
        w_out = jax.random.normal(k4, (DIM, HID // 2), jnp.float32) * (1.0 / np.sqrt(HID // 2))
        return {'x': x, 'fft_filter': fft_filter, 'w_in': w_in, 'w_dw': w_dw, 'w_out': w_out}
    _L1_conv_all = _L1_conv_setup()
    _L1_conv_in = {k: v for k, v in _L1_conv_all.items() if k in ('fft_filter', 'w_in', 'w_dw', 'w_out', )}
    del _L1_conv_all

    return {
        "x": x,
        "L0_conv_Wq": _L0_conv_in["Wq"],
        "L0_conv_bq": _L0_conv_in["bq"],
        "L0_conv_Wk": _L0_conv_in["Wk"],
        "L0_conv_bk": _L0_conv_in["bk"],
        "L0_conv_Wv": _L0_conv_in["Wv"],
        "L0_conv_bv": _L0_conv_in["bv"],
        "L0_conv_Wfc": _L0_conv_in["Wfc"],
        "L0_conv_bfc": _L0_conv_in["bfc"],
        "L1_conv_fft_filter": _L1_conv_in["fft_filter"],
        "L1_conv_w_in": _L1_conv_in["w_in"],
        "L1_conv_w_dw": _L1_conv_in["w_dw"],
        "L1_conv_w_out": _L1_conv_in["w_out"],
    }

def reference(x, L0_conv_Wq, L0_conv_bq, L0_conv_Wk, L0_conv_bk, L0_conv_Wv, L0_conv_bv, L0_conv_Wfc, L0_conv_bfc, L1_conv_fft_filter, L1_conv_w_in, L1_conv_w_dw, L1_conv_w_out):
    import jax
    import jax.numpy as jnp
    def _L0_conv_ref(x, Wq, bq, Wk, bk, Wv, bv, Wfc, bfc):
        import jax, jax.numpy as jnp
        import numpy as np
        THETA = 10000.0
        EMBED_DIM = 384
        NUM_HEADS = 6

        def apply_rope_2d(x):
            B, C, H, W = x.shape
            dim = C // 2
            inv = 1.0 / THETA ** (jnp.arange(0, dim, 2, dtype=x.dtype) / dim)
            fh = jnp.arange(H, dtype=x.dtype)[:, None] * inv[None, :]
            fw = jnp.arange(W, dtype=x.dtype)[:, None] * inv[None, :]
            fh_flat = jnp.broadcast_to(fh[:, None, :], (H, W, dim // 2)).reshape(H * W, dim // 2)
            fw_flat = jnp.broadcast_to(fw[None, :, :], (H, W, dim // 2)).reshape(H * W, dim // 2)
            x_seq = x.reshape(B, C, H * W).transpose(0, 2, 1)
            x_h, x_w = (x_seq[..., :dim], x_seq[..., dim:])

            def apply_rotary(t, f):
                cos = jnp.repeat(jnp.cos(f), 2, axis=-1)
                sin = jnp.repeat(jnp.sin(f), 2, axis=-1)
                t1, t2 = jnp.split(t, 2, axis=-1)
                rot = jnp.concatenate([-t2, t1], axis=-1)
                return t * cos + rot * sin
            x_h = apply_rotary(x_h, fh_flat)
            x_w = apply_rotary(x_w, fw_flat)
            x_out = jnp.concatenate([x_h, x_w], axis=-1)
            return x_out.transpose(0, 2, 1).reshape(B, C, H, W)

        def conv1x1(x, W, b):
            return jnp.einsum('oc,bchw->bohw', W, x) + b[None, :, None, None]
        B, C, H, W = x.shape
        nh = NUM_HEADS
        hd = C // nh
        scale = hd ** (-0.5)
        q = apply_rope_2d(conv1x1(x, Wq, bq))
        k = apply_rope_2d(conv1x1(x, Wk, bk))
        v = conv1x1(x, Wv, bv)

        def to_heads(t):
            return t.reshape(B, nh, hd, H * W).transpose(0, 1, 3, 2)
        q = jax.nn.elu(to_heads(q) * scale) + 1.0
        k = jax.nn.elu(to_heads(k)) + 1.0
        v = to_heads(v)
        kv = jnp.einsum('bhnd,bhne->bhde', k, v)
        k_sum = k.sum(axis=2)
        normalizer = jnp.einsum('bhnd,bhd->bhn', q, k_sum)[..., None]
        out = jnp.einsum('bhnd,bhde->bhne', q, kv) / (normalizer + 1e-06)
        out = out.transpose(0, 1, 3, 2).reshape(B, C, H, W)
        return conv1x1(out, Wfc, bfc)

    def _L1_conv_ref(x, fft_filter, w_in, w_dw, w_out):
        import jax, jax.numpy as jnp
        import numpy as np
        B, DIM, H, W = (2, 384, 256, 256)
        HID = DIM * 1
        P = 8
        b, c, h, w = x.shape
        hid = w_in.shape[0]
        hb, wb = (h // P, w // P)
        t = jnp.einsum('bchw,oc->bohw', x, w_in)
        tp = t.reshape(b, hid, hb, P, wb, P)
        tf = jnp.fft.rfft2(tp, axes=(3, 5))
        tf = tf * fft_filter[None, :, None, :, None, :]
        tp = jnp.fft.irfft2(tf, s=(P, P), axes=(3, 5))
        t = tp.reshape(b, hid, h, w)
        t = jax.lax.conv_general_dilated(t, w_dw, window_strides=(1, 1), padding='SAME', feature_group_count=hid, dimension_numbers=('NCHW', 'OIHW', 'NCHW'))
        x1, x2 = (t[:, :hid // 2], t[:, hid // 2:])
        g = jax.nn.gelu(x1, approximate=False) * x2
        return jnp.einsum('bchw,oc->bohw', g, w_out)

    def _gn(v, G=32, eps=1e-5):
        B_, C_, H_, W_ = v.shape
        g = v.reshape(B_, G, C_ // G, H_, W_)
        m = jnp.mean(g, axis=(2, 3, 4), keepdims=True)
        s = jnp.var(g, axis=(2, 3, 4), keepdims=True)
        return ((g - m) / jnp.sqrt(s + eps)).reshape(v.shape)

    def _ln_c(v, eps=1e-6):
        m = jnp.mean(v, axis=1, keepdims=True)
        s = jnp.var(v, axis=1, keepdims=True)
        return (v - m) / jnp.sqrt(s + eps)

    def _ln_t(v, eps=1e-5):
        m = jnp.mean(v, axis=-1, keepdims=True)
        s = jnp.var(v, axis=-1, keepdims=True)
        return (v - m) / jnp.sqrt(s + eps)

    def _to_tokens(v):
        B_, C_, H_, W_ = v.shape
        return v.reshape(B_, C_, H_ * W_).transpose(0, 2, 1)
    def _from_tokens(t, like):
        B_, C_, H_, W_ = like.shape
        return t.transpose(0, 2, 1).reshape(B_, C_, H_, W_)

    x = x + _L0_conv_ref(_gn(x), L0_conv_Wq, L0_conv_bq, L0_conv_Wk, L0_conv_bk, L0_conv_Wv, L0_conv_bv, L0_conv_Wfc, L0_conv_bfc)
    x = x + _L1_conv_ref(_gn(x), L1_conv_fft_filter, L1_conv_w_in, L1_conv_w_dw, L1_conv_w_out)
    return x


_drawn_inputs = setup_inputs


def setup_inputs(seed=0):
    import zlib

    import numpy as np

    out = dict(_drawn_inputs(seed))
    spreads = {}
    factors = {'L0_conv_Wq': 8.0,
     'L0_conv_bq': 200.0,
     'L0_conv_Wk': 8.0,
     'L0_conv_bk': 200.0,
     'L0_conv_Wv': 8.0,
     'L0_conv_bv': 2.791,
     'L0_conv_Wfc': 2.776}
    for name, (base, spread) in spreads.items():
        noise = np.random.default_rng([zlib.crc32(name.encode()), seed]).standard_normal(out[name].shape)
        drawn = base * np.exp(spread * noise) if base else spread * noise
        out[name] = jnp.asarray(drawn.astype(out[name].dtype))
    for name, factor in factors.items():
        out[name] = (out[name] * factor).astype(out[name].dtype)
    return out
```

```python
import math

import numpy as np
import concourse.bass as bass
from concourse import mybir
from contextlib import ExitStack

B, C, H, W = 8, 384, 64, 64
NTOK = H * W
P = 128
KB = C // P
CHUNK = 512
NCH = NTOK // CHUNK
ROWS = CHUNK // W
TPC = CHUNK // P
NT = NCH * TPC
HEADS, HD = 6, 64
HALF = C // 2
ROT = HALF // 2
GROUP = C // 32
PATCH = 8
HP, WP = H + 2, W + 2
TAPS = 9
GN_EPS = 1e-5
NORM_EPS = 1e-6
THETA = 10000.0
GBLOCKS = [(k, m) for m in range(KB) for k in range(KB) if abs(k - m) <= 1]


def rotary_tables():
    inv = (np.float32(1.0) / np.float32(THETA) ** (np.arange(0, HALF, 2, dtype=np.float32) / np.float32(HALF))).astype(np.float32)
    part = np.arange(P)
    rows = (np.arange(NT)[None, :] * (P // W) + part[:, None] // W).astype(np.float32)
    cols = (part % W).astype(np.float32)
    ang_h = (rows[:, :, None] * inv).astype(np.float32).astype(np.float64)
    ang_w = (cols[:, None] * inv).astype(np.float32).astype(np.float64)
    nf = ROT // 2

    def source_sin(ang):
        s = np.sin(ang)
        return np.concatenate([s[..., nf:], -s[..., :nf]], axis=-1)

    f32 = np.float32
    return (np.cos(ang_h).astype(f32), source_sin(ang_h).astype(f32),
            np.cos(ang_w).astype(f32), source_sin(ang_w).astype(f32))


def patch_basis():
    n = PATCH
    r, s = np.meshgrid(np.arange(n), np.arange(n), indexing="ij")
    funcs, picks = [], []
    for u in range(n):
        for v in range(n // 2 + 1):
            if v in (0, n // 2):
                if u > n // 2:
                    continue
                pick = np.zeros((n, n // 2 + 1))
                pick[u, v] += 0.5
                pick[(-u) % n, v] += 0.5
            else:
                pick = np.zeros((n, n // 2 + 1))
                pick[u, v] = 1.0
            ang = 2 * np.pi * ((u * r + v * s) % n) / n
            for f in (np.cos(ang), np.sin(ang)):
                norm = np.sqrt((f ** 2).sum())
                if norm > 1e-6:
                    funcs.append(f / norm)
                    picks.append(pick.ravel())
    funcs, picks = np.array(funcs), np.array(picks)
    assert len(funcs) == n * n
    phi = np.zeros((P, P))
    sel = np.zeros((P, P))
    for pp in range(2):
        for k in range(n * n):
            for rr in range(n):
                phi[rr * 16 + pp * 8:rr * 16 + pp * 8 + 8, pp * 64 + k] = funcs[k][rr]
            sel[:n * (n // 2 + 1), pp * 64 + k] = picks[k]
    return phi.astype(np.float32), sel.astype(np.float32)


def constants():
    cos_h, sin_h, cos_w, sin_w = rotary_tables()
    phi, sel = patch_basis()
    g = np.kron(np.eye(C // GROUP), np.full((GROUP, GROUP), 1.0 / GROUP)).astype(np.float32)
    gavg = np.stack([g[k * P:(k + 1) * P, m * P:(m + 1) * P] for k, m in GBLOCKS], axis=1)
    rowpick = np.zeros((P, 2), np.float32)
    rowpick[0, 0] = 1.0
    rowpick[1, 1] = 1.0
    return {
        "cos_h": cos_h, "sin_h": sin_h,
        "cs_w": np.stack([cos_w, sin_w], axis=1),
        "mats": np.stack([np.eye(P, dtype=np.float32),
                          np.kron(np.eye(2), np.ones((HD, HD))).astype(np.float32),
                          phi, np.ascontiguousarray(phi.T), sel], axis=1),
        "gavg": np.ascontiguousarray(gavg),
        "rowpick": rowpick,
    }


def build_program(nc, x, wqkv_t, bqk, bv, wfc_t, bfc, filt, w_in_t, w_dw, w_out_t,
                  cos_h, sin_h, cs_w, mats, gavg, rowpick, out, images=B):
    fp32, fp32r = mybir.dt.float32, mybir.dt.float32r
    ALU, ACT, AX = mybir.AluOpType, mybir.ActivationFunctionType, mybir.AxisListType
    ds = bass.ds

    x_v = x.rearrange("b (k p) (c n) -> b p k c n", p=P, n=CHUNK)
    out_v = out.rearrange("b (k p) (c n) -> b p k c n", p=P, n=CHUNK)
    x1_dram = nc.dram_tensor("x1_scratch", (images, C, NTOK), fp32, kind="Internal").ap()
    x1_v = x1_dram.rearrange("b (k p) (c n) -> b p k c n", p=P, n=CHUNK)

    ctx = ExitStack()
    with ctx:
        def sb(name, shape, dt=fp32):
            return ctx.enter_context(nc.sbuf_tensor(name, shape, dt))

        def sem(name):
            return ctx.enter_context(nc.semaphore(name))

        t_cosh = sb("t_cosh", [P, NT, ROT])
        t_sinh = sb("t_sinh", [P, NT, ROT])
        t_csw = sb("t_csw", [P, 2, ROT])
        t_mats = sb("t_mats", [P, 5, P])
        ident, headmask, phi, phi_t, sel = (t_mats[:, j, :] for j in range(5))
        t_gavg = sb("t_gavg", [P, len(GBLOCKS), P])
        t_rowpick = sb("t_rowpick", [P, 2])
        ones_f = sb("ones_f", [P, P])
        ones_r = sb("ones_r", [P, P], fp32r)
        w_hi = sb("w_hi", [P, KB, 3 * C], fp32r)
        w_lo = sb("w_lo", [P, KB, 3 * C], fp32r)
        qkbias = sb("qkbias", [P, 2 * C], fp32r)
        bv_bc = sb("bv_bc", [P, C])
        wfc = sb("wfc", [P, KB, C])
        bfc_c = sb("bfc_c", [P, KB])
        win_hi = sb("win_hi", [P, KB, C], fp32r)
        win_lo = sb("win_lo", [P, KB, C], fp32r)
        wdw = sb("wdw", [P, KB, TAPS])
        wout = sb("wout", [P, 2, C])
        fsel = sb("fsel", [P, C])
        bn_x = sb("bn_x", [P, KB, NCH, 6])
        bn_x1 = sb("bn_x1", [P, KB, NCH, 6])
        mv = sb("mv", [P, 2, KB, 2])
        dev = sb("dev", [P, 2, KB])
        gmean = sb("gmean", [P, 2, KB])
        gvar = sb("gvar", [P, 2, KB])
        gstd = sb("gstd", [P, 2, KB])
        rstd = sb("rstd", [P, 2, KB])
        newt = sb("newt", [P, 2, KB])
        counted = sb("counted", [P, 32])
        ksum = sb("ksum", [P, KB])
        nrm = sb("nrm", [P, TPC * HEADS])
        big = sb("big", [P, KB * HP * WP])
        q_all = big[:, 0:NT * C].rearrange("p (t c) -> p t c", c=C)
        filt_img = big[:, :].rearrange("p (k y z) -> p k y z", k=KB, z=WP)
        xa = sb("xa", [P, 2, KB, CHUNK])
        xr = sb("xr", [P, 2, KB, CHUNK])

        def overlay(*variants):
            made = []
            for variant in variants[:-1]:
                with ExitStack() as inner:
                    made.append([inner.enter_context(nc.sbuf_tensor(n, s, d)) for n, s, d in variant])
            made.append([sb(n, s, d) for n, s, d in variants[-1]])
            return made

        (kvfix, kdiag, kv_t, kbc, mout, qt), (x_hi, x_lo) = overlay(
            [("kvfix", [P, KB, P], fp32), ("kdiag", [P, KB, P], fp32), ("kv_t", [P, KB, P], fp32),
             ("kbc", [P, C], fp32), ("mout", [P, KB, C], fp32), ("qt", [P, 2, KB, CHUNK], fp32)],
            [("x_hi", [P, 2, KB, CHUNK], fp32r), ("x_lo", [P, 2, KB, CHUNK], fp32r)])
        (w_raw, ), (qn, ), (t1, t2, kt), (tb, gb, acc, gel) = overlay(
            [("w_raw", [P, KB, 3 * C], fp32)],
            [("qn", [P, 2, TPC, C], fp32)],
            [("t1", [P, 2, 2, 2, HALF], fp32), ("t2", [P, 2, 2, 2, HALF], fp32), ("kt", [P, 2, C], fp32)],
            [("tb", [P, 2, C], fp32), ("gb", [P, 2, C], fp32), ("acc", [P, KB, CHUNK], fp32),
             ("gel", [P, 2, CHUNK], fp32)])
        vt = sb("vt", [P, 2, KB, P + 1])

        bank = [ctx.enter_context(nc.psum_tensor(f"bank{j}", [P, 512], fp32)) for j in range(8)]
        KVB = 6

        s_init = sem("s_init")
        s_cst = sem("s_cst")
        s_raw = sem("s_raw")
        s_setup_a = sem("s_setup_a")
        s_setup_v = sem("s_setup_v")
        s_setup_p = sem("s_setup_p")
        s_fz = sem("s_fz")
        s_xa = [sem(f"s_xa{j}") for j in range(2)]
        s_xr = [sem(f"s_xr{j}") for j in range(2)]
        s_st = [sem(f"s_st{j}") for j in range(2)]
        s_stat = sem("s_stat")
        s_x1s = sem("s_x1s")
        s_nrm = sem("s_nrm")
        s_hi = sem("s_hi")
        s_lo = sem("s_lo")
        s_xfree = sem("s_xfree")
        s_qkv = sem("s_qkv")
        s_rope = sem("s_rope")
        s_add = sem("s_add")
        s_exp = sem("s_exp")
        s_elu = sem("s_elu")
        s_v = sem("s_v")
        s_kv = sem("s_kv")
        s_kd = sem("s_kd")
        s_kp = sem("s_kp")
        s_ka = sem("s_ka")
        s_prod = sem("s_prod")
        s_nd = sem("s_nd")
        s_qn = sem("s_qn")
        s_tp = sem("s_tp")
        s_qt = sem("s_qt")
        s_out = sem("s_out")
        s_res = sem("s_res")
        s_gs = sem("s_gs")
        s_gp = sem("s_gp")
        s_ga = sem("s_ga")
        s_tm = sem("s_tm")
        s_t = sem("s_t")
        s_dft = sem("s_dft")
        s_f = sem("s_f")
        s_inv = sem("s_inv")
        s_img = sem("s_img")
        s_brd = sem("s_brd")
        s_dw = sem("s_dw")
        s_gel = sem("s_gel")
        s_gate = sem("s_gate")

        s_past = sem("s_past")

        AHEAD = {s_lo: 2, s_xfree: 2, s_rope: 2, s_v: 2, s_kv: 2, s_tp: 6, s_qt: 2, s_res: 2, s_t: 2,
                 s_dft: 2, s_f: 2, s_inv: 2, s_img: 2, s_x1s: 2, s_out: 6, s_elu: 2, s_qn: 1,
                 s_gate: 1, s_st[0]: 16, s_st[1]: 16}

        def steps(eng, total, lo, hi, body):
            for c in range(lo):
                body(c, c // 2, c, c % 2)
            with eng.Fori(0, (hi - lo) // 2) as k:
                for u in range(2):
                    body(k * 2 + (lo + u), k + (lo + u) // 2, None, (lo + u) % 2)
            for c in range(hi, total):
                body(c, c // 2, c, c % 2)

        def within(edge, a, b, off=0):
            return edge is None or a <= edge + off < b

        def chunk_of(view, i, c):
            return view[ds(i, 1), :, :, ds(c, 1), :].rearrange("b p k c n -> (b p) k (c n)")

        SPLIT = [(0, HALF, HD ** -0.5), (HALF, 2 * HALF, 1.0), (2 * HALF, 3 * HALF, HD ** -0.5),
                 (3 * HALF, 4 * HALF, 1.0), (4 * HALF, 6 * HALF, 1.0)]
        NCST = 12

        def by_patches(ap):
            return ap.rearrange("p (r w s) -> p w r s", r=ROWS, s=16)

        block = ctx.enter_context(nc.Block())

        @block.sync
        def _(sp):
            sp.dma_start(w_raw[:, :, :], wqkv_t.rearrange("(k p) n -> p k n", p=P)).then_inc(s_raw, 16)
            for dst, src in ((t_cosh, cos_h), (t_sinh, sin_h), (t_csw, cs_w), (t_mats, mats), (t_gavg, gavg),
                             (t_rowpick, rowpick), (bfc_c, bfc), (wdw, w_dw), (wout, w_out_t)):
                sp.dma_start(dst[:], src).then_inc(s_cst, 16)
            sp.dma_start(bv_bc[:], bv[0:1, :].to_broadcast([P, C])).then_inc(s_cst, 16)
            sp.dma_start(wfc[:], wfc_t.rearrange("(k p) n -> p k n", p=P)).then_inc(s_cst, 16)
            sp.wait_ge(s_init, 1)
            sp.dma_start(fsel[0:filt.shape[0], :], filt).then_inc(s_cst, 16)
            for c in range(NCH):
                if c >= 2:
                    sp.wait_ge(s_stat, c - 1)
                sp.dma_start(xa[:, c % 2], x_v[0, :, :, c, :]).then_inc(s_xa[c % 2], 16)
            sp.wait_ge(s_setup_v, 1)
            sp.dma_start(w_raw[:, :, 0:C], w_in_t.rearrange("(k p) n -> p k n", p=P)).then_inc(s_raw, 16)
            sp.dma_start(w_raw[:, 0, C:3 * C], bqk[0:1, :].to_broadcast([P, 2 * C])).then_inc(s_raw, 16)
            sp.wait_ge(s_stat, NCH)

            def wait(sem, value):
                sp.wait_ge(sem, value)
                sp.sem_inc(s_past, 1)

            with sp.Fori(0, images) as i:
                def load_a(c, h, edge, par):
                    wait(s_lo, i * 16 + c + 1)
                    sp.dma_start(xa[:, par], chunk_of(x_v, i, c)).then_inc(s_xa[par], 16)
                steps(sp, NCH, 0, NCH, load_a)

                wait(s_lo, i * 16 + (NCH + 2))

                def part_b(c, h, edge, par):
                    if within(edge, 0, NCH):
                        wait(s_stat, i * 8 + c + (NCH - 1))
                        sp.dma_start(xa[:, par], chunk_of(x_v, (i + 1) & (images - 1), c)).then_inc(s_xa[par], 16)
                    if within(edge, 0, NCH, -2):
                        wait(s_res, (i * 16 + c) * 3 - 1)
                        sp.dma_start(chunk_of(x1_v, i, c - 2), xr[:, par]).then_inc(s_st[par], 16)
                    if within(edge, 0, NCH):
                        wait(s_x1s, i * 8 + c + 1)
                        wait(s_st[par], (i * 8 + h + 1) * 16)
                        sp.dma_start(xr[:, par], chunk_of(x_v, i, c)).then_inc(s_xr[par], 16)
                steps(sp, NCH + 2, 2, NCH, part_b)

                wait(s_stat, i * 8 + 2 * NCH)
                wait(s_x1s, i * 8 + (NCH + 2))

                def load_c(c, h, par):
                    wait(s_lo, i * 16 + c + (NCH + 1))
                    wait(s_st[par], (i * 8 + h + 2) * 16)
                    sp.dma_start(xa[:, par], chunk_of(x1_v, i, c)).then_inc(s_xa[par], 16)
                load_c(0, 0, 0)
                load_c(1, 0, 1)

                def part_c(c, h, edge, par):
                    if within(edge, 0, NCH, 2):
                        load_c(c + 2, h + 1, par)
                    if within(edge, 0, NCH, -2):
                        wait(s_res, (i * 16 + c + NCH) * 3 - 1)
                        sp.dma_start(chunk_of(out_v, i, c - 2), xr[:, par]).then_inc(s_st[par], 16)
                    if within(edge, 0, NCH):
                        wait(s_st[par], (i * 8 + h + 5) * 16)
                        sp.dma_start(xr[:, par], chunk_of(x1_v, i, c)).then_inc(s_xr[par], 16)
                steps(sp, NCH + 2, 2, NCH - 2, part_c)
            for par in range(2):
                wait(s_st[par], (images * 8 + 1) * 16)

        @block.gpsimd
        def _(gp):
            nc.gpsimd.memset(fsel[:], 0.0)
            nc.gpsimd.memset(ones_f[:], 1.0)
            nc.gpsimd.memset(vt[:, :, :, P:P + 1], 1.0)
            for j, (s, n) in enumerate(AHEAD.items()):
                nc.gpsimd.memset(counted[:, j:j + 1], 0.0).then_inc(s, n)
            nc.gpsimd.memset(counted[:, len(AHEAD):], 0.0).then_inc(s_init, 1)

            def low_part(m, k, par, patches=False):
                if k == 0:
                    gp.wait_ge(s_hi, m + 1)
                dst, src, hi = x_lo[:, par, k], xa[:, par, k], x_hi[:, par, k].bitcast(fp32)
                if patches:
                    dst, hi = (ap.rearrange("p (w r s) -> p w r s", r=ROWS, s=16) for ap in (dst, hi))
                    src = by_patches(src)
                ins = nc.gpsimd.tensor_tensor(dst, src, hi, ALU.subtract)
                if k == KB - 1:
                    ins.then_inc(s_lo, 1)

            def rotated_sum(T, p2):
                gp.wait_ge(s_rope, T + 3)
                a = t1[:, p2].rearrange("p b s (t f) -> p (b s) t f", t=2)
                b = t2[:, p2].rearrange("p b s (t f) -> p (b s) t f", t=2)
                nc.gpsimd.tensor_tensor(a, a, b[:, :, ::-1, :], ALU.add).then_inc(s_add, 1)

            with gp.Fori(0, images) as i:
                for k in range(KB):
                    low_part(i * 16, k, 0)
                rotated_sum(i * NT, 0)

                def part_a(c, h, edge, par):
                    T = (i * 8 + c) * 4
                    for j in range(TPC):
                        if j < KB and within(edge, 0, NCH, 1):
                            low_part(i * 16 + c + 1, j, 1 - par)
                        if j < TPC - 1 or within(edge, 0, NCH, 1):
                            rotated_sum(T + j + 1, (j + 1) % 2)
                steps(gp, NCH, 0, NCH - 2, part_a)

                gp.wait_ge(s_ka, i * 3 + 1)
                gp.sem_inc(s_past, 1)

                def part_b(c, h, edge, par):
                    n = i * 8 + c
                    gp.wait_ge(s_tp, n * 3 + 3)
                    nc.gpsimd.tensor_tensor(qn[:, par], q_all[:, ds(c * 4, 4), :],
                                            kbc[:, :].unsqueeze(1).to_broadcast([P, TPC, C]), ALU.mult)\
                        .then_inc(s_prod, 1)
                steps(gp, NCH, 0, NCH, part_b)

                gp.wait_ge(s_qn, i * NCH + (NCH + 1))
                gp.sem_inc(s_past, 1)
                nc.gpsimd.memset(filt_img[:, :, 0:HP:HP - 1, :], 0.0)
                nc.gpsimd.memset(filt_img[:, :, 1:HP - 1, 0:WP:WP - 1], 0.0).then_inc(s_brd, 1)
                for k in range(KB):
                    low_part(i * 16 + NCH, k, 0, patches=True)

                def part_c(c, h, edge, par):
                    for k in range(KB):
                        low_part(i * 16 + c + (NCH + 1), k, 1 - par, patches=True)
                steps(gp, NCH - 1, 0, NCH - 2, part_c)

        @block.scalar
        def _(act):
            act.wait_ge(s_init, 1)

            def high_part(m, par, patches=False):
                act.wait_ge(s_nrm, m + 1)
                act.wait_ge(s_xfree, m + 1)
                if patches:
                    for k in range(KB):
                        ins = nc.scalar.activation(x_hi[:, par, k].rearrange("p (w r s) -> p w r s", r=ROWS, s=16),
                                                   by_patches(xa[:, par, k]), ACT.Copy)
                else:
                    ins = nc.scalar.activation(x_hi[:, par], xa[:, par], ACT.Copy)
                ins.then_inc(s_hi, 1)

            def tile_a(T, p2):
                act.wait_ge(s_add, T + 1)
                nc.scalar.activation(t2[:, p2], t1[:, p2], ACT.Exp).then_inc(s_exp, 1)
                act.wait_ge(s_qkv, T * 3 + 3)
                act.wait_ge(s_kv, T + 1)
                nc.scalar.activation(vt[:, p2, :, 0:P], bank[3 * p2 + 2][:, 0:C].rearrange("p (k n) -> p k n", k=KB),
                                     ACT.Copy).then_inc(s_v, 1)
                act.wait_ge(s_exp, T * 2 + 1)
                nc.scalar.activation(t1[:, p2], t1[:, p2], ACT.Relu).then_inc(s_exp, 1)

            def group_root(f):
                act.wait_ge(s_gs, f * 10 + 5)
                nc.scalar.activation(gstd[:, :, :], gvar[:, :, :], ACT.Sqrt).then_inc(s_ga, 1)

            group_root(0)
            with act.Fori(0, images) as i:
                high_part(i * 16, 0)
                tile_a(i * NT, 0)

                def part_a(c, h, edge, par):
                    T = (i * 8 + c) * 4
                    for j in range(TPC):
                        if j == 0 and within(edge, 0, NCH, 1):
                            high_part(i * 16 + c + 1, 1 - par)
                        if j < TPC - 1 or within(edge, 0, NCH, 1):
                            tile_a(T + j + 1, (j + 1) % 2)
                steps(act, NCH, 0, NCH - 2, part_a)

                act.wait_ge(s_kp, i * 5 + 1)
                nc.scalar.activation(kbc[:, :], bank[0][:, 0:C], ACT.Copy).then_inc(s_ka, 1)
                act.wait_ge(s_kp, i * 5 + 2)
                nc.scalar.activation(kv_t[:, :, :], bank[1][:, 0:C].rearrange("p (k n) -> p k n", k=KB), ACT.Copy)\
                    .then_inc(s_ka, 1)
                for j in range(KB):
                    act.wait_ge(s_kp, i * 5 + 3 + j)
                    ins = nc.scalar.activation(mout[:, j], bank[2 + j][:, 0:C], ACT.Copy)
                ins.then_inc(s_ka, 1)

                def part_b(c, h, edge, par):
                    n = i * 8 + c
                    act.wait_ge(s_out, (i * 16 + c) * 3 + 3)
                    for j in range(KB):
                        act.wait_ge(s_tp, n * 3 + (j + 7))
                        ins = nc.scalar.activation(qt[:, par, j], bank[3 * par + j][:, :], ACT.Copy)
                    ins.then_inc(s_qt, 1)
                steps(act, NCH, 0, NCH, part_b)
                group_root(i + 1)

                def copy_t(T, p2):
                    act.wait_ge(s_tm, T + 1)
                    act.wait_ge(s_dft, T + 1)
                    nc.scalar.activation(tb[:, p2], bank[p2][:, 0:C], ACT.Copy).then_inc(s_t, 1)

                def copy_img(T, c, j):
                    act.wait_ge(s_inv, T + 3)
                    dst = filt_img[:, :, ds(c * ROWS + 1, ROWS), 1 + 16 * j:17 + 16 * j]
                    src = bank[4 + j % 2][:, 0:C].rearrange("p (k r s) -> p k r s", k=KB, s=16)
                    nc.scalar.activation(dst, src, ACT.Copy).then_inc(s_img, 1)

                def gelus(c):
                    n = i * 8 + c
                    act.wait_ge(s_dw, n * 27 + 25)
                    act.wait_ge(s_out, (i * 16 + c) * 3 + 3 * (NCH + 2))
                    nc.scalar.activation(gel[:, 0], acc[:, 0], ACT.Gelu).then_inc(s_gel, 1)
                    act.wait_ge(s_dw, n * 27 + 27)
                    nc.scalar.activation(gel[HD:P, 1], acc[0:HD, 2], ACT.Gelu).then_inc(s_gel, 1)

                high_part(i * 16 + NCH, 0, patches=True)

                def part_c(c, h, edge, par):
                    T = (i * 8 + c) * 4
                    if within(edge, 0, NCH):
                        copy_t(T, 0)
                        copy_t(T + 1, 1)
                        copy_t(T + 2, 0)
                        copy_img(T, c, 0)
                        copy_t(T + 3, 1)
                        copy_img(T + 1, c, 1)
                        if within(edge, 0, NCH, 1):
                            high_part(i * 16 + c + (NCH + 1), 1 - par, patches=True)
                        copy_img(T + 2, c, 2)
                        copy_img(T + 3, c, 3)
                    if within(edge, 0, NCH, -1):
                        gelus(c - 1)
                steps(act, NCH + 1, 1, NCH - 1, part_c)

        @block.vector
        def _(dve):
            dve.wait_ge(s_init, 1)
            nc.vector.tensor_copy(ones_r[:], ones_f[:])
            nc.vector.memset(bn_x1[:], 1.0)
            nc.vector.memset(gvar[:], 1.0)
            dve.wait_ge(s_raw, 16)
            count = [0]

            def link(ins):
                count[0] += 1
                ins.then_inc(s_setup_p, 1)
                dve.wait_ge(s_setup_p, count[0])

            def split(hi, lo, raw, scale):
                link(nc.vector.tensor_scalar(hi, raw, scale, None, ALU.mult))
                return nc.vector.scalar_tensor_tensor(lo, raw, scale, hi.bitcast(fp32), ALU.mult, ALU.subtract)

            for a, b, scale in SPLIT:
                ins = split(w_hi[:, :, a:b], w_lo[:, :, a:b], w_raw[:, :, a:b], scale)
            ins.then_inc(s_setup_v, 1)

            def x_stats(h, par, c):
                dve.wait_ge(s_xa[par], h * 16)
                for k in range(KB):
                    ins = nc.vector.bn_stats(bn_x[:, k, ds(c, 1), :].rearrange("p c s -> p (c s)"), xa[:, par, k])
                ins.then_inc(s_stat, 1)

            for c in range(NCH):
                x_stats(c // 2 + 1, c % 2, c)

            dve.wait_ge(s_raw, 48)
            link(split(win_hi[:], win_lo[:], w_raw[:, :, 0:C], 1.0))
            dve.wait_ge(s_cst, NCST * 16)
            for a, b, scale in SPLIT[:4]:
                hi, raw = qkbias[:, a:b], w_raw[:, 0, C + a:C + b]
                tmp = w_raw[:, 1, C + a:C + b]
                link(split(hi, tmp, raw, scale))
                link(nc.vector.tensor_scalar(tmp, tmp, t_rowpick[:, 1:2], None, ALU.mult))
                ins = nc.vector.scalar_tensor_tensor(hi, hi.bitcast(fp32), t_rowpick[:, 0:1], tmp, ALU.mult, ALU.add)
            ins.then_inc(s_setup_v, 1)
            dve.wait_ge(s_setup_a, 1)
            nc.vector.tensor_copy(fsel[:], bank[0][:, 0:C]).then_inc(s_setup_v, 1)

            def group_norm(f):
                g = f * 10

                def nxt(ins, k):
                    ins.then_inc(s_gs, 1)
                    dve.wait_ge(s_gs, g + k)

                dve.wait_ge(s_stat, f * NCH + NCH)
                dve.wait_ge(s_x1s, f * NCH + 2)
                dve.sem_inc(s_past, 1)
                for s, bn in enumerate((bn_x, bn_x1)):
                    for k in range(KB):
                        ins = nc.vector.bn_aggr(mv[:, s, k], bn[:, k].rearrange("p c s -> p (c s)"))
                nxt(ins, 1)
                dve.wait_ge(s_gp, f * 2 + 1)
                pm = bank[7][:, 0:2 * KB].rearrange("p (m s) -> p s m", s=2)
                nc.vector.tensor_copy(gmean[:, :, :], pm)
                nxt(nc.vector.tensor_tensor(dev[:, :, :], mv[:, :, :, 0], pm, ALU.subtract), 2)
                nxt(nc.vector.tensor_tensor(newt[:, :, :], dev[:, :, :], dev[:, :, :], ALU.mult), 3)
                nxt(nc.vector.tensor_tensor(dev[:, :, :], newt[:, :, :], mv[:, :, :, 1], ALU.add), 4)
                dve.wait_ge(s_gp, f * 2 + 2)
                nxt(nc.vector.tensor_scalar(gvar[:, :, :], pm, GN_EPS, None, ALU.add), 5)
                dve.wait_ge(s_ga, f + 1)
                nxt(nc.vector.reciprocal(rstd[:, :, :], gstd[:, :, :]), 6)
                nxt(nc.vector.tensor_tensor(newt[:, :, :], rstd[:, :, :], rstd[:, :, :], ALU.mult), 7)
                nxt(nc.vector.tensor_tensor(newt[:, :, :], newt[:, :, :], gvar[:, :, :], ALU.mult), 8)
                nxt(nc.vector.tensor_scalar(newt[:, :, :], newt[:, :, :], -0.5, 1.5, ALU.mult, ALU.add), 9)
                nxt(nc.vector.tensor_tensor(rstd[:, :, :], rstd[:, :, :], newt[:, :, :], ALU.mult), 10)

            group_norm(0)

            def normalise(s, loads, par):
                dve.wait_ge(s_xa[par], loads * 16)
                for k in range(KB):
                    ins = nc.vector.tensor_scalar(xa[:, par, k], xa[:, par, k], gmean[:, s, k:k + 1],
                                                  rstd[:, s, k:k + 1], ALU.subtract, ALU.mult)
                ins.then_inc(s_nrm, 1)

            def rope(T, tile, p2):
                wide = [P, 2, ROT, 2]
                dve.wait_ge(s_elu, T + 1)
                tabs = [(t_cosh[:, ds(tile, 1), :].rearrange("p a f -> p (a f)"),
                         t_sinh[:, ds(tile, 1), :].rearrange("p a f -> p (a f)")),
                        (t_csw[:, 0, :], t_csw[:, 1, :])]
                for b in range(2):
                    dve.wait_ge(s_qkv, T * 3 + (b + 1))
                    src = bank[3 * p2 + b][:, 0:C].rearrange("p (s f r) -> p s f r", s=2, r=2)
                    for dst, tab in zip((t1, t2), tabs[b]):
                        ins = nc.vector.tensor_tensor(dst[:, p2, b].rearrange("p s (f r) -> p s f r", r=2), src,
                                                      tab.unsqueeze(1).unsqueeze(3).to_broadcast(wide), ALU.mult)
                ins.then_inc(s_rope, 1)

            def elu(T, tile, p2):
                dve.wait_ge(s_exp, T * 2 + 2)
                dve.wait_ge(s_kv, T + 1)
                qdst = q_all[:, ds(tile, 1), :].rearrange("p a (b f) -> p (a b) f", b=2)
                for s, dst in enumerate((qdst, kt[:, p2].rearrange("p (b f) -> p b f", b=2))):
                    ins = nc.vector.scalar_tensor_tensor(dst, t2[:, p2, :, s], 1.0, t1[:, p2, :, s], ALU.min, ALU.add)
                ins.then_inc(s_elu, 1)

            with dve.Fori(0, images) as i:
                normalise(0, i * 12 + 5, 0)
                rope(i * NT, 0, 0)

                def part_a(c, h, edge, par):
                    T = (i * 8 + c) * 4
                    if within(edge, 0, NCH, 1):
                        normalise(0, i * 12 + 5 + h + par, 1 - par)
                    for j in range(TPC):
                        if j < TPC - 1 or within(edge, 0, NCH, 1):
                            rope(T + j + 1, c * 4 + (j + 1), (j + 1) % 2)
                        elu(T + j, c * 4 + j, j % 2)
                steps(dve, NCH, 0, NCH - 2, part_a)

                kvp = bank[KVB][:, 0:KB * (P + 1)].rearrange("p (k n) -> p k n", k=KB)
                dve.wait_ge(s_kv, i * NT + (NT + 2))
                nc.vector.tensor_copy(ksum[:, :], kvp[:, :, P]).then_inc(s_kd, 1)
                dve.wait_ge(s_kd, i * 4 + 1)
                for j in range(KB):
                    ins = nc.vector.tensor_scalar(kdiag[:, j], ident, ksum[:, j:j + 1], None, ALU.mult)
                ins.then_inc(s_kd, 1)
                for j in range(KB):
                    ins = nc.vector.scalar_tensor_tensor(kvfix[:, j], bv_bc[:, j * P:(j + 1) * P], ksum[:, j:j + 1],
                                                         kvp[:, j, 0:P], ALU.mult, ALU.add)
                ins.then_inc(s_kd, 1)
                dve.wait_ge(s_kd, i * 4 + 3)
                nc.vector.tensor_tensor(kvfix[:, :, :], kvfix[:, :, :], headmask.unsqueeze(1).to_broadcast([P, KB, P]),
                                        ALU.mult).then_inc(s_kd, 1)

                def divide_q(c, par):
                    n = i * 8 + c
                    by_head = qn[:, par].rearrange("p t (h d) -> p (t h) d", d=HD)
                    dve.wait_ge(s_prod, n + 1)
                    dve.wait_ge(s_qn, n + 1)
                    nc.vector.tensor_reduce(nrm[:, :], by_head, AX.X, ALU.add).then_inc(s_nd, 1)
                    dve.wait_ge(s_nd, n * 3 + 1)
                    nc.vector.tensor_scalar(nrm[:, :], nrm[:, :], NORM_EPS, None, ALU.add).then_inc(s_nd, 1)
                    dve.wait_ge(s_nd, n * 3 + 2)
                    nc.vector.reciprocal(nrm[:, :], nrm[:, :]).then_inc(s_nd, 1)
                    dve.wait_ge(s_nd, n * 3 + 3)
                    nc.vector.tensor_tensor(by_head, q_all[:, ds(c * 4, 4), :].rearrange("p t (h d) -> p (t h) d", d=HD),
                                            nrm[:, :].unsqueeze(2).to_broadcast([P, TPC * HEADS, HD]), ALU.mult)\
                        .then_inc(s_qn, 1)

                def residual(r, loads, par, bias):
                    dve.wait_ge(s_xr[par], loads * 16)
                    for m in range(KB):
                        dve.wait_ge(s_out, r * 3 + (m + 7))
                        ps = bank[6 + (par + m) % 2][:, :]
                        if bias:
                            ins = nc.vector.scalar_tensor_tensor(xr[:, par, m], ps, bfc_c[:, m:m + 1], xr[:, par, m],
                                                                 ALU.add, ALU.add)
                        else:
                            ins = nc.vector.tensor_tensor(xr[:, par, m], ps, xr[:, par, m], ALU.add)
                        ins.then_inc(s_res, 1)

                divide_q(0, 0)

                def part_b(c, h, edge, par):
                    if within(edge, 0, NCH, 1):
                        divide_q(c + 1, 1 - par)
                    residual(i * 16 + c, i * 8 + h + 1, par, True)
                    x_stats(i * 12 + 9 + h, par, c)
                    dve.wait_ge(s_res, (i * 16 + c) * 3 + 5)
                    for k in range(KB):
                        ins = nc.vector.bn_stats(bn_x1[:, k, ds(c, 1), :].rearrange("p c s -> p (c s)"), xr[:, par, k])
                    ins.then_inc(s_x1s, 1)
                steps(dve, NCH, 0, NCH - 2, part_b)
                group_norm(i + 1)

                def times_filter(T, p2):
                    dve.wait_ge(s_dft, T + 3)
                    dve.wait_ge(s_inv, T + 1)
                    nc.vector.tensor_tensor(gb[:, p2], bank[2 + p2][:, 0:C], fsel[:, :], ALU.mult).then_inc(s_f, 1)

                ORDER = [(dy, dx) for dy in (-1, 0, 1) for dx in (-1, 0, 1)]

                def depthwise(c, q0, q1):
                    n = i * 8 + c
                    for q in range(q0, q1):
                        (dy, dx), k = ORDER[q // KB], q % KB
                        src = filt_img[:, k, ds(c * ROWS + (1 + dy), ROWS), 1 + dx:1 + dx + W]
                        tap = wdw[:, k, q // KB:q // KB + 1]
                        dst = acc[:, k].rearrange("p (r s) -> p r s", s=W)
                        if q < KB:
                            if q == 0:
                                dve.wait_ge(s_gate, n + 1)
                            ins = nc.vector.tensor_scalar(dst, src, tap, None, ALU.mult)
                        else:
                            dve.wait_ge(s_dw, n * 27 + (q - KB + 1))
                            ins = nc.vector.scalar_tensor_tensor(dst, src, tap, dst, ALU.mult, ALU.add)
                        ins.then_inc(s_dw, 1)

                def gate(c):
                    n = i * 8 + c
                    dve.wait_ge(s_dw, n * 27 + 27)
                    dve.wait_ge(s_gel, n * 2 + 1)
                    nc.vector.tensor_tensor(gel[:, 0], gel[:, 0], acc[:, 1], ALU.mult)
                    dve.wait_ge(s_gel, n * 2 + 2)
                    nc.vector.tensor_tensor(gel[HD:P, 1], gel[HD:P, 1], acc[HD:P, 2], ALU.mult).then_inc(s_gate, 1)

                normalise(1, i * 12 + 13, 0)
                dve.wait_ge(s_brd, i + 1)

                def part_c(c, h, edge, par):
                    T = (i * 8 + c) * 4
                    tile, conv = within(edge, 0, NCH), within(edge, 0, NCH, -1)
                    if tile:
                        times_filter(T, 0)
                    if conv:
                        dve.wait_ge(s_img, T + 2)
                        depthwise(c - 1, 0, 6)
                    if tile:
                        times_filter(T + 1, 1)
                        if within(edge, 0, NCH, 1):
                            normalise(1, i * 12 + 13 + h + par, 1 - par)
                    if conv:
                        depthwise(c - 1, 6, 12)
                    if tile:
                        times_filter(T + 2, 0)
                    if conv:
                        depthwise(c - 1, 12, 18)
                    if tile:
                        times_filter(T + 3, 1)
                    if within(edge, 0, NCH, -2):
                        residual(i * 16 + c + (NCH - 2), i * 8 + 4 + h, par, False)
                    if conv:
                        if tile:
                            dve.wait_ge(s_img, T + 6)
                        depthwise(c - 1, 18, 27)
                        gate(c - 1)
                steps(dve, NCH + 2, 2, NCH - 2, part_c)

        @block.tensor
        def _(pe):
            pe.wait_ge(s_init, 1)
            pe.wait_ge(s_cst, NCST * 16)
            nc.tensor.matmul(bank[0][:, 0:C], sel, fsel[:, :], start=True, stop=True).then_inc(s_setup_a, 1)

            def group_avg(f):
                for step, (wait, src) in enumerate(((1, lambda k: mv[:, :, k, 0]), (4, lambda k: dev[:, :, k]))):
                    pe.wait_ge(s_gs, f * 10 + wait)
                    for m in range(KB):
                        ks = [k for k, mm in GBLOCKS if mm == m]
                        for k in ks:
                            ins = nc.tensor.matmul(bank[7][:, 2 * m:2 * m + 2], t_gavg[:, GBLOCKS.index((k, m)), :], src(k),
                                                   start=(k == ks[0]), stop=(k == ks[-1]))
                    ins.then_inc(s_gp, 1)

            group_avg(0)
            pe.wait_ge(s_setup_v, 3)

            def split_product(dst, hi, lo, whi, wlo, first=True, last=True):
                pairs = [(hi(k), w) for k in range(KB) for w in (whi(k), wlo(k))] + [(lo(k), whi(k)) for k in range(KB)]
                for q, (a, b) in enumerate(pairs):
                    ins = nc.tensor.matmul(dst, a, b, start=first and q == 0, stop=last and q == len(pairs) - 1)
                return ins

            def project(T, m, par, j):
                p2 = j % 2
                pe.wait_ge(s_hi, m + 1)
                pe.wait_ge(s_lo, m + 3)
                pe.wait_ge(s_rope, T + 1)
                pe.wait_ge(s_v, T + 1)
                tok = slice(j * P, (j + 1) * P)
                for b in range(3):
                    dst = bank[3 * p2 + b][:, 0:C]
                    cols = slice(b * C, (b + 1) * C)
                    if b < 2:
                        nc.tensor.matmul(dst, ones_r[:, :], qkbias[:, cols], start=True, stop=False)
                    ins = split_product(dst, lambda k: x_hi[:, par, k, tok], lambda k: x_lo[:, par, k, tok],
                                        lambda k: w_hi[:, k, cols], lambda k: w_lo[:, k, cols], first=(b == 2))
                    ins.then_inc(s_qkv, 1)

            def add_kv(T, j, first=False, last=False, frees=False):
                pe.wait_ge(s_elu, T + 3)
                pe.wait_ge(s_v, T + 3)
                p2 = j % 2
                for k in range(KB):
                    ins = nc.tensor.matmul(bank[KVB][:, k * (P + 1):(k + 1) * (P + 1)], kt[:, p2, k * P:(k + 1) * P],
                                           vt[:, p2, k, :], start=(first and k == 0), stop=last, skip_group_check=True)
                    if frees and k == 0:
                        ins.then_inc(s_xfree, 1)
                ins.then_inc(s_kv, 1)

            with pe.Fori(0, images) as i:
                pe.wait_ge(s_res, i * 48 + 2)
                pe.wait_ge(s_img, i * NT + 2)
                pe.wait_ge(s_f, i * NT + 2)
                pe.wait_ge(s_t, i * NT + 2)
                project(i * NT, i * 16, 0, 0)
                project(i * NT + 1, i * 16, 0, 1)

                def part_a(c, h, edge, par):
                    T = (i * 8 + c) * 4
                    first = edge == 0
                    m = i * 16 + c
                    project(T + 2, m, par, 2)
                    add_kv(T, 0, first=first)
                    project(T + 3, m, par, 3)
                    add_kv(T + 1, 1, frees=True)
                    if within(edge, 0, NCH, 1):
                        project(T + 4, m + 1, 1 - par, 0)
                    add_kv(T + 2, 2)
                    if within(edge, 0, NCH, 1):
                        project(T + 5, m + 1, 1 - par, 1)
                    add_kv(T + 3, 3, last=(edge == NCH - 1))

                steps(pe, NCH, 2, NCH - 2, part_a)

                pe.wait_ge(s_kd, i * 4 + 2)
                nc.tensor.matmul(bank[0][:, 0:C], ones_f[:, :], kdiag[:, :, :], start=True, stop=True).then_inc(s_kp, 1)
                pe.wait_ge(s_kd, i * 4 + 4)
                for j in range(KB):
                    ins = nc.tensor.transpose(bank[1][:, j * P:(j + 1) * P], kvfix[:, j], ident)
                ins.then_inc(s_kp, 1)
                pe.wait_ge(s_ka, i * 3 + 2)
                for j in range(KB):
                    nc.tensor.matmul(bank[2 + j][:, 0:C], kv_t[:, j], wfc[:, j], start=True, stop=True).then_inc(s_kp, 1)
                pe.wait_ge(s_ka, i * 3 + 3)

                def transpose_q(c, par):
                    n = i * 8 + c
                    pe.wait_ge(s_qn, n + 2)
                    pe.wait_ge(s_qt, n + 1)
                    for j in range(KB):
                        for u in range(TPC):
                            ins = nc.tensor.transpose(bank[3 * par + j][:, u * P:(u + 1) * P],
                                                      qn[:, par, u, j * P:(j + 1) * P], ident)
                        ins.then_inc(s_tp, 1)

                transpose_q(0, 0)

                def part_b(c, h, edge, par):
                    pe.wait_ge(s_qt, i * 8 + c + 3)
                    r = (i * 16 + c) * 3
                    for m in range(KB):
                        if m == KB - 1 and within(edge, 0, NCH, 1):
                            transpose_q(c + 1, 1 - par)
                        pe.wait_ge(s_res, r + (m + 1))
                        for j in range(KB):
                            ins = nc.tensor.matmul(bank[6 + (par + m) % 2][:, :], mout[:, j, m * P:(m + 1) * P],
                                                   qt[:, par, j], start=(j == 0), stop=(j == KB - 1))
                        ins.then_inc(s_out, 1)
                steps(pe, NCH, 0, NCH - 2, part_b)
                group_avg(i + 1)

                pe.wait_ge(s_res, i * 48 + (3 * NCH + 2))

                def t_tile(T, m, par, j):
                    p2 = j % 2
                    pe.wait_ge(s_hi, m + 1)
                    pe.wait_ge(s_lo, m + 3)
                    pe.wait_ge(s_t, T + 1)

                    pix = slice(j * P, (j + 1) * P)
                    split_product(bank[p2][:, 0:C], lambda k: x_hi[:, par, k, pix], lambda k: x_lo[:, par, k, pix],
                                  lambda k: win_hi[:, k], lambda k: win_lo[:, k]).then_inc(s_tm, 1)

                def dft_tile(T, j, frees=False):
                    p2 = j % 2
                    pe.wait_ge(s_t, T + 3)
                    pe.wait_ge(s_f, T + 1)
                    nc.tensor.matmul(bank[2 + p2][:, 0:C], phi, tb[:, p2], start=True, stop=True).then_inc(s_dft, 1)

                def inverse_tile(T, j, frees=False):
                    p2 = j % 2
                    pe.wait_ge(s_f, T + 3)
                    pe.wait_ge(s_img, T + 1)
                    for k in range(KB):
                        ins = nc.tensor.matmul(bank[4 + p2][:, k * P:(k + 1) * P], gb[:, p2, k * P:(k + 1) * P], phi_t,
                                               start=True, stop=True)
                        if frees and k == 0:
                            ins.then_inc(s_xfree, 1)
                    ins.then_inc(s_inv, 1)

                def out_block(c, m, par):
                    pe.wait_ge(s_gate, i * 8 + c + 2)
                    pe.wait_ge(s_res, (i * 16 + c + NCH) * 3 + (m + 1))
                    dst = bank[6 + (par + m) % 2][:, :]
                    nc.tensor.matmul(dst, wout[:, 0, m * P:(m + 1) * P], gel[:, 0], start=True, stop=False)
                    nc.tensor.matmul(dst, wout[HD:P, 1, m * P:(m + 1) * P], gel[HD:P, 1], start=False, stop=True)\
                        .then_inc(s_out, 1)

                def part_c(c, h, edge, par):
                    T = (i * 8 + c) * 4
                    m = i * 16 + c + NCH
                    tile, prod = within(edge, 0, NCH), within(edge, 0, NCH, -2)
                    if tile:
                        t_tile(T, m, par, 0)
                        t_tile(T + 1, m, par, 1)
                        dft_tile(T, 0)
                        t_tile(T + 2, m, par, 2)
                        dft_tile(T + 1, 1)
                        inverse_tile(T, 0)
                    if prod:
                        out_block(c - 2, 0, par)
                    if tile:
                        t_tile(T + 3, m, par, 3)
                        dft_tile(T + 2, 2)
                        inverse_tile(T + 1, 1, frees=True)
                    if prod:
                        out_block(c - 2, 1, par)
                    if tile:
                        dft_tile(T + 3, 3)
                        inverse_tile(T + 2, 2)
                    if prod:
                        out_block(c - 2, 2, par)
                    if tile:
                        inverse_tile(T + 3, 3)
                steps(pe, NCH + 2, 2, NCH, part_c)


def kernel(x, L0_conv_Wq, L0_conv_bq, L0_conv_Wk, L0_conv_bk, L0_conv_Wv, L0_conv_bv, L0_conv_Wfc, L0_conv_bfc,
           L1_conv_fft_filter, L1_conv_w_in, L1_conv_w_dw, L1_conv_w_out):
    import concourse.bacc as bacc
    from concourse.bass_utils import run_bass_kernel_spmd

    a = np.asarray
    images = x.shape[0]
    wq, wk, wv = a(L0_conv_Wq).T, a(L0_conv_Wk).T, a(L0_conv_Wv).T
    bq, bk = a(L0_conv_bq), a(L0_conv_bk)
    half = C // 2
    order = np.concatenate([np.arange(P), half + np.arange(P), np.arange(P, half), half + np.arange(P, half)])
    wo = a(L1_conv_w_out).T
    wout = np.zeros((P, 2, C), wo.dtype)
    wout[:, 0] = wo[:P]
    wout[HD:, 1] = wo[P:]
    arrays = {
        "x": a(x).reshape(images, C, NTOK),
        "wqkv_t": np.concatenate([wq[:, :HALF], wk[:, :HALF], wq[:, HALF:], wk[:, HALF:], wv], axis=1),
        "bqk": np.concatenate([bq[:HALF], bk[:HALF], bq[HALF:], bk[HALF:]])[None],
        "bv": a(L0_conv_bv)[None],
        "wfc_t": a(L0_conv_Wfc).T,
        "bfc": a(L0_conv_bfc).reshape(KB, P).T,
        "filt": a(L1_conv_fft_filter)[order].reshape(C, -1).T,
        "w_in_t": a(L1_conv_w_in)[order].T,
        "w_dw": a(L1_conv_w_dw)[order].reshape(KB, P, TAPS).transpose(1, 0, 2),
        "w_out_t": wout,
    }
    arrays.update(constants())
    arrays = {k: np.ascontiguousarray(v) for k, v in arrays.items()}
    nc = bacc.Bacc("TRN2", target_bir_lowering=False, num_devices=1)
    aps = {k: nc.dram_tensor(k, v.shape, mybir.dt.from_np(v.dtype), kind="ExternalInput").ap() for k, v in arrays.items()}
    out = nc.dram_tensor("out", (images, C, NTOK), mybir.dt.float32, kind="ExternalOutput").ap()
    build_program(nc, **aps, out=out, images=images)
    r = run_bass_kernel_spmd(nc, [arrays], core_ids=[0])
    return r.results[0]["out"].reshape(images, C, H, W)
```

```python
import math

import numpy as np
import concourse.bass as bass
from concourse import mybir
from contextlib import ExitStack

B, C, H, W = 8, 384, 64, 64
NTOK = H * W
P = 128
KB = C // P
CHUNK = 512
NCH = NTOK // CHUNK
ROWS = CHUNK // W
TPC = CHUNK // P
NT = NCH * TPC
HEADS, HD = 6, 64
HALF = C // 2
ROT = HALF // 2
GROUP = C // 32
PATCH = 8
HP, WP = H + 2, W + 2
TAPS = 9
GN_EPS = 1e-5
NORM_EPS = 1e-6
THETA = 10000.0
GBLOCKS = [(k, m) for m in range(KB) for k in range(KB) if abs(k - m) <= 1]


def rotary_tables():
    inv = (np.float32(1.0) / np.float32(THETA) ** (np.arange(0, HALF, 2, dtype=np.float32) / np.float32(HALF))).astype(np.float32)
    part = np.arange(P)
    rows = (np.arange(NT)[None, :] * (P // W) + part[:, None] // W).astype(np.float32)
    cols = (part % W).astype(np.float32)
    ang_h = (rows[:, :, None] * inv).astype(np.float32).astype(np.float64)
    ang_w = (cols[:, None] * inv).astype(np.float32).astype(np.float64)
    nf = ROT // 2

    def source_sin(ang):
        s = np.sin(ang)
        return np.concatenate([s[..., nf:], -s[..., :nf]], axis=-1)

    f32 = np.float32
    return (np.cos(ang_h).astype(f32), source_sin(ang_h).astype(f32),
            np.cos(ang_w).astype(f32), source_sin(ang_w).astype(f32))


def patch_basis():
    n = PATCH
    r, s = np.meshgrid(np.arange(n), np.arange(n), indexing="ij")
    funcs, picks = [], []
    for u in range(n):
        for v in range(n // 2 + 1):
            if v in (0, n // 2):
                if u > n // 2:
                    continue
                pick = np.zeros((n, n // 2 + 1))
                pick[u, v] += 0.5
                pick[(-u) % n, v] += 0.5
            else:
                pick = np.zeros((n, n // 2 + 1))
                pick[u, v] = 1.0
            ang = 2 * np.pi * ((u * r + v * s) % n) / n
            for f in (np.cos(ang), np.sin(ang)):
                norm = np.sqrt((f ** 2).sum())
                if norm > 1e-6:
                    funcs.append(f / norm)
                    picks.append(pick.ravel())
    funcs, picks = np.array(funcs), np.array(picks)
    assert len(funcs) == n * n
    phi = np.zeros((P, P))
    sel = np.zeros((P, P))
    for pp in range(2):
        for k in range(n * n):
            for rr in range(n):
                phi[rr * 16 + pp * 8:rr * 16 + pp * 8 + 8, pp * 64 + k] = funcs[k][rr]
            sel[:n * (n // 2 + 1), pp * 64 + k] = picks[k]
    return phi.astype(np.float32), sel.astype(np.float32)


def constants():
    cos_h, sin_h, cos_w, sin_w = rotary_tables()
    phi, sel = patch_basis()
    g = np.kron(np.eye(C // GROUP), np.full((GROUP, GROUP), 1.0 / GROUP)).astype(np.float32)
    gavg = np.stack([g[k * P:(k + 1) * P, m * P:(m + 1) * P] for k, m in GBLOCKS], axis=1)
    rowpick = np.zeros((P, 2), np.float32)
    rowpick[0, 0] = 1.0
    rowpick[1, 1] = 1.0
    return {
        "cos_h": cos_h, "sin_h": sin_h,
        "cs_w": np.stack([cos_w, sin_w], axis=1),
        "mats": np.stack([np.eye(P, dtype=np.float32),
                          np.kron(np.eye(2), np.ones((HD, HD))).astype(np.float32),
                          phi, np.ascontiguousarray(phi.T), sel], axis=1),
        "gavg": np.ascontiguousarray(gavg),
        "rowpick": rowpick,
    }


def build_program(nc, x, wqkv_t, bqk, bv, wfc_t, bfc, filt, w_in_t, w_dw, w_out_t,
                  cos_h, sin_h, cs_w, mats, gavg, rowpick, out, images=B):
    fp32, fp32r = mybir.dt.float32, mybir.dt.float32r
    ALU, ACT, AX = mybir.AluOpType, mybir.ActivationFunctionType, mybir.AxisListType
    ds = bass.ds

    x_v = x.rearrange("b (k p) (c n) -> b p k c n", p=P, n=CHUNK)
    out_v = out.rearrange("b (k p) (c n) -> b p k c n", p=P, n=CHUNK)
    x1_dram = nc.dram_tensor("x1_scratch", (images, C, NTOK), fp32, kind="Internal").ap()
    x1_v = x1_dram.rearrange("b (k p) (c n) -> b p k c n", p=P, n=CHUNK)

    ctx = ExitStack()
    with ctx:
        def sb(name, shape, dt=fp32):
            return ctx.enter_context(nc.sbuf_tensor(name, shape, dt))

        def sem(name):
            return ctx.enter_context(nc.semaphore(name))

        t_cosh = sb("t_cosh", [P, NT, ROT])
        t_sinh = sb("t_sinh", [P, NT, ROT])
        t_csw = sb("t_csw", [P, 2, ROT])
        t_mats = sb("t_mats", [P, 5, P])
        ident, headmask, phi, phi_t, sel = (t_mats[:, j, :] for j in range(5))
        t_gavg = sb("t_gavg", [P, len(GBLOCKS), P])
        t_rowpick = sb("t_rowpick", [P, 2])
        ones_f = sb("ones_f", [P, P])
        ones_r = sb("ones_r", [P, P], fp32r)
        w_hi = sb("w_hi", [P, KB, 3 * C], fp32r)
        w_lo = sb("w_lo", [P, KB, 3 * C], fp32r)
        qkbias = sb("qkbias", [P, 2 * C], fp32r)
        bv_bc = sb("bv_bc", [P, C])
        wfc = sb("wfc", [P, KB, C])
        bfc_c = sb("bfc_c", [P, KB])
        win_hi = sb("win_hi", [P, KB, C], fp32r)
        win_lo = sb("win_lo", [P, KB, C], fp32r)
        wdw = sb("wdw", [P, KB, TAPS])
        wout = sb("wout", [P, 2, C])
        fsel = sb("fsel", [P, C])
        bn_x = sb("bn_x", [P, KB, NCH, 6])
        bn_x1 = sb("bn_x1", [P, KB, NCH, 6])
        mv = sb("mv", [P, 2, KB, 2])
        dev = sb("dev", [P, 2, KB])
        gmean = sb("gmean", [P, 2, KB])
        gvar = sb("gvar", [P, 2, KB])
        gstd = sb("gstd", [P, 2, KB])
        rstd = sb("rstd", [P, 2, KB])
        newt = sb("newt", [P, 2, KB])
        shift = sb("shift", [P, 2, KB])
        counted = sb("counted", [P, 32])
        ksum = sb("ksum", [P, KB])
        nrm = sb("nrm", [P, TPC * HEADS])
        big = sb("big", [P, KB * HP * WP])
        q_all = big[:, 0:NT * C].rearrange("p (t c) -> p t c", c=C)
        filt_img = big[:, :].rearrange("p (k y z) -> p k y z", k=KB, z=WP)
        xa = sb("xa", [P, 2, KB, CHUNK])
        xr = sb("xr", [P, 2, KB, CHUNK])

        def overlay(*variants):
            made = []
            for variant in variants[:-1]:
                with ExitStack() as inner:
                    made.append([inner.enter_context(nc.sbuf_tensor(n, s, d)) for n, s, d in variant])
            made.append([sb(n, s, d) for n, s, d in variants[-1]])
            return made

        (kvfix, kdiag, kv_t, kbc, mout, qt), (x_hi, x_lo) = overlay(
            [("kvfix", [P, KB, P], fp32), ("kdiag", [P, KB, P], fp32), ("kv_t", [P, KB, P], fp32),
             ("kbc", [P, C], fp32), ("mout", [P, KB, C], fp32), ("qt", [P, 2, KB, CHUNK], fp32)],
            [("x_hi", [P, 2, KB, CHUNK], fp32r), ("x_lo", [P, 2, KB, CHUNK], fp32r)])
        (w_raw, ), (qn, ), (t1, t2, kt), (tb, gb, acc, gel) = overlay(
            [("w_raw", [P, KB, 3 * C], fp32)],
            [("qn", [P, 2, TPC, C], fp32)],
            [("t1", [P, 2, 2, 2, HALF], fp32), ("t2", [P, 2, 2, 2, HALF], fp32), ("kt", [P, 2, C], fp32)],
            [("tb", [P, 2, C], fp32), ("gb", [P, 2, C], fp32), ("acc", [P, KB, CHUNK], fp32),
             ("gel", [P, 2, CHUNK], fp32)])
        vt = sb("vt", [P, 2, KB, P + 1])

        bank = [ctx.enter_context(nc.psum_tensor(f"bank{j}", [P, 512], fp32)) for j in range(8)]
        KVB = 6

        s_init = sem("s_init")
        s_cst = sem("s_cst")
        s_raw = sem("s_raw")
        s_setup_a = sem("s_setup_a")
        s_setup_v = sem("s_setup_v")
        s_setup_p = sem("s_setup_p")
        s_fz = sem("s_fz")
        s_xa = [sem(f"s_xa{j}") for j in range(2)]
        s_xr = [sem(f"s_xr{j}") for j in range(2)]
        s_st = [sem(f"s_st{j}") for j in range(2)]
        s_stat = sem("s_stat")
        s_x1s = sem("s_x1s")
        s_nrm = sem("s_nrm")
        s_hi = sem("s_hi")
        s_lo = sem("s_lo")
        s_xfree = sem("s_xfree")
        s_qkv = sem("s_qkv")
        s_rope = sem("s_rope")
        s_add = sem("s_add")
        s_exp = sem("s_exp")
        s_elu = sem("s_elu")
        s_v = sem("s_v")
        s_kv = sem("s_kv")
        s_kd = sem("s_kd")
        s_kp = sem("s_kp")
        s_ka = sem("s_ka")
        s_prod = sem("s_prod")
        s_nd = sem("s_nd")
        s_qn = sem("s_qn")
        s_tp = sem("s_tp")
        s_qt = sem("s_qt")
        s_out = sem("s_out")
        s_res = sem("s_res")
        s_gs = sem("s_gs")
        s_gp = sem("s_gp")
        s_ga = sem("s_ga")
        s_tm = sem("s_tm")
        s_t = sem("s_t")
        s_dft = sem("s_dft")
        s_f = sem("s_f")
        s_inv = sem("s_inv")
        s_img = sem("s_img")
        s_brd = sem("s_brd")
        s_tap = sem("s_tap")
        s_dw = sem("s_dw")
        s_gel = sem("s_gel")
        s_gate = sem("s_gate")

        s_past = sem("s_past")

        AHEAD = {s_lo: 6, s_xfree: 2, s_rope: 2, s_v: 2, s_kv: 2, s_tp: 6, s_qt: 2, s_res: 6, s_t: 2,
                 s_dft: 2, s_f: 2, s_inv: 2, s_img: 2, s_x1s: 2, s_out: 6, s_elu: 2, s_qn: 1,
                 s_gate: 2, s_gel: 2, s_st[0]: 16, s_st[1]: 16}

        def steps(eng, total, lo, hi, body):
            for c in range(lo):
                body(c, c // 2, c, c % 2)
            with eng.Fori(0, (hi - lo) // 2) as k:
                for u in range(2):
                    body(k * 2 + (lo + u), k + (lo + u) // 2, None, (lo + u) % 2)
            for c in range(hi, total):
                body(c, c // 2, c, c % 2)

        def within(edge, a, b, off=0):
            return edge is None or a <= edge + off < b

        def chunk_of(view, i, c):
            return view[ds(i, 1), :, :, ds(c, 1), :].rearrange("b p k c n -> (b p) k (c n)")

        SPLIT = [(0, HALF, HD ** -0.5), (HALF, 2 * HALF, 1.0), (2 * HALF, 3 * HALF, HD ** -0.5),
                 (3 * HALF, 4 * HALF, 1.0), (4 * HALF, 6 * HALF, 1.0)]
        NCST = 12

        def by_patches(ap):
            return ap.rearrange("p (r w s) -> p w r s", r=ROWS, s=16)

        def out_bank(m, tail):
            return 6 + m % 2 if tail else 5 + m

        block = ctx.enter_context(nc.Block())

        @block.sync
        def _(sp):
            sp.dma_start(w_raw[:, :, :], wqkv_t.rearrange("(k p) n -> p k n", p=P)).then_inc(s_raw, 16)
            for dst, src in ((t_cosh, cos_h), (t_sinh, sin_h), (t_csw, cs_w), (t_mats, mats), (t_gavg, gavg),
                             (t_rowpick, rowpick), (bfc_c, bfc), (wdw, w_dw), (wout, w_out_t)):
                sp.dma_start(dst[:], src).then_inc(s_cst, 16)
            sp.dma_start(bv_bc[:], bv[0:1, :].to_broadcast([P, C])).then_inc(s_cst, 16)
            sp.dma_start(wfc[:], wfc_t.rearrange("(k p) n -> p k n", p=P)).then_inc(s_cst, 16)
            sp.wait_ge(s_init, 1)
            sp.dma_start(fsel[0:filt.shape[0], :], filt).then_inc(s_cst, 16)
            for c in range(NCH):
                if c >= 2:
                    sp.wait_ge(s_stat, c - 1)
                sp.dma_start(xa[:, c % 2], x_v[0, :, :, c, :]).then_inc(s_xa[c % 2], 16)
            sp.wait_ge(s_setup_v, 1)
            sp.dma_start(w_raw[:, :, 0:C], w_in_t.rearrange("(k p) n -> p k n", p=P)).then_inc(s_raw, 16)
            sp.dma_start(w_raw[:, 0, C:3 * C], bqk[0:1, :].to_broadcast([P, 2 * C])).then_inc(s_raw, 16)
            sp.wait_ge(s_stat, NCH)
            for c in range(2):
                sp.dma_start(xa[:, c], x_v[0, :, :, c, :]).then_inc(s_xa[c], 16)

            def wait(sem, value):
                sp.wait_ge(sem, value)
                sp.sem_inc(s_past, 1)

            with sp.Fori(0, images) as i:
                def load_a(c, h, edge, par):
                    wait(s_lo, (i * 16 + c) * 3 + 9)
                    sp.dma_start(xa[:, par], chunk_of(x_v, i, c + 2)).then_inc(s_xa[par], 16)
                steps(sp, NCH - 2, 0, NCH - 2, load_a)

                wait(s_lo, (i * 16 + NCH) * 3 + 6)

                def part_b(c, h, edge, par):
                    if within(edge, 0, NCH):
                        wait(s_stat, i * 8 + c + (NCH - 1))
                        sp.dma_start(xa[:, par], chunk_of(x_v, (i + 1) & (images - 1), c)).then_inc(s_xa[par], 16)
                    if within(edge, 0, NCH, -2):
                        wait(s_res, (i * 16 + c) * 3 + 3)
                        sp.dma_start(chunk_of(x1_v, i, c - 2), xr[:, par]).then_inc(s_st[par], 16)
                    if within(edge, 0, NCH):
                        wait(s_x1s, i * 8 + c + 1)
                        wait(s_st[par], (i * 8 + h + 1) * 16)
                        sp.dma_start(xr[:, par], chunk_of(x_v, i, c)).then_inc(s_xr[par], 16)
                steps(sp, NCH + 2, 2, NCH, part_b)

                wait(s_stat, i * 8 + 2 * NCH)
                wait(s_x1s, i * 8 + (NCH + 2))

                def load_c(c, h, par):
                    wait(s_lo, (i * 16 + c + NCH) * 3 + 3)
                    wait(s_st[par], (i * 8 + h + 2) * 16)
                    sp.dma_start(xa[:, par], chunk_of(x1_v, i, c)).then_inc(s_xa[par], 16)
                load_c(0, 0, 0)
                load_c(1, 0, 1)

                def part_c(c, h, edge, par):
                    if within(edge, 0, NCH, 2):
                        load_c(c + 2, h + 1, par)
                    if edge in (NCH - 2, NCH - 1):
                        wait(s_lo, (i * 16 + c + (NCH + 2)) * 3 + 3)
                        sp.dma_start(xa[:, par], chunk_of(x_v, (i + 1) & (images - 1), c - (NCH - 2)))\
                            .then_inc(s_xa[par], 16)
                    if within(edge, 0, NCH, -2):
                        wait(s_res, (i * 16 + c + NCH) * 3 + 3)
                        sp.dma_start(chunk_of(out_v, i, c - 2), xr[:, par]).then_inc(s_st[par], 16)
                    if within(edge, 0, NCH):
                        wait(s_st[par], (i * 8 + h + 5) * 16)
                        sp.dma_start(xr[:, par], chunk_of(x1_v, i, c)).then_inc(s_xr[par], 16)
                steps(sp, NCH + 2, 2, NCH - 2, part_c)
            for par in range(2):
                wait(s_xa[par], (images * 12 + 5) * 16)
                wait(s_st[par], (images * 8 + 1) * 16)

        @block.gpsimd
        def _(gp):
            nc.gpsimd.memset(fsel[:], 0.0)
            nc.gpsimd.memset(ones_f[:], 1.0)
            nc.gpsimd.memset(vt[:, :, :, P:P + 1], 1.0)
            for j, (s, n) in enumerate(AHEAD.items()):
                nc.gpsimd.memset(counted[:, j:j + 1], 0.0).then_inc(s, n)
            nc.gpsimd.memset(counted[:, len(AHEAD):], 0.0).then_inc(s_init, 1)

            def low_part(m, k, par, patches=False):
                gp.wait_ge(s_hi, m * 3 + (k + 1))
                dst, src, hi = x_lo[:, par, k], xa[:, par, k], x_hi[:, par, k].bitcast(fp32)
                if patches:
                    dst, hi = (ap.rearrange("p (w r s) -> p w r s", r=ROWS, s=16) for ap in (dst, hi))
                    src = by_patches(src)
                nc.gpsimd.tensor_tensor(dst, src, hi, ALU.subtract).then_inc(s_lo, 1)

            def rotated_sum(T, p2):
                gp.wait_ge(s_rope, T + 3)
                a = t1[:, p2].rearrange("p b s (t f) -> p (b s) t f", t=2)
                b = t2[:, p2].rearrange("p b s (t f) -> p (b s) t f", t=2)
                nc.gpsimd.tensor_tensor(a, a, b[:, :, ::-1, :], ALU.add).then_inc(s_add, 1)

            for k in range(KB):
                low_part(0, k, 0)
            with gp.Fori(0, images) as i:
                rotated_sum(i * NT, 0)

                def part_a(c, h, edge, par):
                    T = (i * 8 + c) * 4
                    for j in range(TPC):
                        if j < KB and within(edge, 0, NCH, 1):
                            low_part(i * 16 + c + 1, j, 1 - par)
                        if j < TPC - 1 or within(edge, 0, NCH, 1):
                            rotated_sum(T + j + 1, (j + 1) % 2)
                steps(gp, NCH, 0, NCH - 2, part_a)

                gp.wait_ge(s_ka, i * 3 + 1)
                gp.sem_inc(s_past, 1)

                def part_b(c, h, edge, par):
                    n = i * 8 + c
                    gp.wait_ge(s_tp, n * 3 + 3)
                    nc.gpsimd.tensor_tensor(qn[:, par], q_all[:, ds(c * 4, 4), :],
                                            kbc[:, :].unsqueeze(1).to_broadcast([P, TPC, C]), ALU.mult)\
                        .then_inc(s_prod, 1)
                steps(gp, NCH, 0, NCH, part_b)

                gp.wait_ge(s_qn, i * NCH + (NCH + 1))
                gp.sem_inc(s_past, 1)
                nc.gpsimd.memset(filt_img[:, :, 0:HP:HP - 1, :], 0.0)
                nc.gpsimd.memset(filt_img[:, :, 1:HP - 1, 0:WP:WP - 1], 0.0).then_inc(s_brd, 1)
                for k in range(KB):
                    low_part(i * 16 + NCH, k, 0, patches=True)

                def part_c(c, h, edge, par):
                    for k in range(KB):
                        low_part(i * 16 + c + (NCH + 1), k, 1 - par, patches=True)
                steps(gp, NCH - 1, 0, NCH - 2, part_c)
                for k in range(KB):
                    low_part(i * 16 + 16, k, 0)

        @block.scalar
        def _(act):
            act.wait_ge(s_init, 1)

            def normalise(loads, par):
                act.wait_ge(s_xa[par], loads * 16)
                for k in range(KB):
                    nc.scalar.activation(xa[:, par, k], xa[:, par, k], ACT.Identity, bias=shift[:, 1, k:k + 1],
                                         scale=rstd[:, 1, k:k + 1]).then_inc(s_nrm, 1)

            def high_part(m, par, patches=False):
                act.wait_ge(s_xfree, m + 1)
                for k in range(KB):
                    act.wait_ge(s_nrm, m * 3 + (k + 1))
                    dst, src = x_hi[:, par, k], xa[:, par, k]
                    if patches:
                        dst, src = dst.rearrange("p (w r s) -> p w r s", r=ROWS, s=16), by_patches(src)
                    nc.scalar.activation(dst, src, ACT.Copy).then_inc(s_hi, 1)

            def tile_a(T, p2):
                act.wait_ge(s_add, T + 1)
                nc.scalar.activation(t2[:, p2], t1[:, p2], ACT.Exp).then_inc(s_exp, 1)
                act.wait_ge(s_qkv, T * 3 + 3)
                act.wait_ge(s_kv, T + 1)
                nc.scalar.activation(vt[:, p2, :, 0:P], bank[3 * p2 + 2][:, 0:C].rearrange("p (k n) -> p k n", k=KB),
                                     ACT.Copy).then_inc(s_v, 1)
                act.wait_ge(s_exp, T * 2 + 1)
                nc.scalar.activation(t1[:, p2], t1[:, p2], ACT.Relu).then_inc(s_exp, 1)

            def group_root(f):
                act.wait_ge(s_gs, f * 11 + 5)
                nc.scalar.activation(gstd[:, :, :], gvar[:, :, :], ACT.Sqrt).then_inc(s_ga, 1)

            group_root(0)
            high_part(0, 0)
            with act.Fori(0, images) as i:
                tile_a(i * NT, 0)

                def part_a(c, h, edge, par):
                    T = (i * 8 + c) * 4
                    for j in range(TPC):
                        if j == 0 and within(edge, 0, NCH, 1):
                            high_part(i * 16 + c + 1, 1 - par)
                        if j < TPC - 1 or within(edge, 0, NCH, 1):
                            tile_a(T + j + 1, (j + 1) % 2)
                steps(act, NCH, 0, NCH - 2, part_a)

                act.wait_ge(s_kp, i * 5 + 1)
                nc.scalar.activation(kbc[:, :], bank[0][:, 0:C], ACT.Copy).then_inc(s_ka, 1)
                act.wait_ge(s_kp, i * 5 + 2)
                nc.scalar.activation(kv_t[:, :, :], bank[1][:, 0:C].rearrange("p (k n) -> p k n", k=KB), ACT.Copy)\
                    .then_inc(s_ka, 1)
                for j in range(KB):
                    act.wait_ge(s_kp, i * 5 + 3 + j)
                    ins = nc.scalar.activation(mout[:, j], bank[2 + j][:, 0:C], ACT.Copy)
                ins.then_inc(s_ka, 1)

                def part_b(c, h, edge, par):
                    n = i * 8 + c
                    act.wait_ge(s_out, (i * 16 + c) * 3 + 3)
                    for j in range(KB):
                        act.wait_ge(s_tp, n * 3 + (j + 7))
                        nc.scalar.activation(qt[:, par, j], bank[(par + j) % 2][:, :], ACT.Copy).then_inc(s_qt, 1)
                steps(act, NCH, 0, NCH, part_b)
                group_root(i + 1)

                def copy_t(T, p2):
                    act.wait_ge(s_tm, T + 1)
                    act.wait_ge(s_dft, T + 1)
                    nc.scalar.activation(tb[:, p2], bank[p2][:, 0:C], ACT.Copy).then_inc(s_t, 1)

                def copy_img(T, c, j):
                    act.wait_ge(s_inv, T + 3)
                    dst = filt_img[:, :, ds(c * ROWS + 1, ROWS), 1 + 16 * j:17 + 16 * j]
                    src = bank[4][:, 0:C].rearrange("p (k r s) -> p k r s", k=KB, s=16)
                    nc.scalar.activation(dst, src, ACT.Copy).then_inc(s_img, 1)

                def gelu(c, m):
                    n = i * 8 + c
                    act.wait_ge(s_dw, n * 24 + (22 + 2 * m))
                    if m == 0:
                        act.wait_ge(s_out, (i * 16 + c) * 3 + 3 * (NCH + 2))
                        nc.scalar.activation(gel[:, 0], acc[:, 0], ACT.Gelu).then_inc(s_gel, 1)
                    else:
                        nc.scalar.activation(gel[HD:P, 1], acc[0:HD, 2], ACT.Gelu).then_inc(s_gel, 1)

                def first_tap(c, k):
                    if k == 0:
                        act.wait_ge(s_img, (i * 8 + c) * 4 + 6)
                        act.wait_ge(s_gel, (i * 8 + c) * 2 + 1)
                    else:
                        act.wait_ge(s_gate, (i * 8 + c) * 2 + k)
                    nc.scalar.activation(acc[:, k].rearrange("p (r s) -> p r s", s=W),
                                         filt_img[:, k, ds(c * ROWS, ROWS), 0:W], ACT.Copy, scale=wdw[:, k, 0:1])\
                        .then_inc(s_tap, 1)

                act.wait_ge(s_gs, (i + 1) * 11 + 11)
                act.wait_ge(s_brd, i + 1)
                act.sem_inc(s_past, 1)
                for u in range(2):
                    high_part(i * 16 + (NCH + u), u, patches=True)

                def part_c(c, h, edge, par):
                    T = (i * 8 + c) * 4
                    tile, conv, gated = (within(edge, 0, NCH, -d) for d in range(3))
                    if tile:
                        copy_t(T, 0)
                    if gated:
                        gelu(c - 2, 0)
                    if conv and edge != 1:
                        first_tap(c - 1, 0)
                    if tile:
                        copy_t(T + 1, 1)
                    if gated:
                        gelu(c - 2, 1)
                    if edge == NCH:
                        high_part(i * 16 + 16, 0)
                    if conv and edge != 1:
                        first_tap(c - 1, 1)
                        first_tap(c - 1, 2)
                    if tile:
                        copy_t(T + 2, 0)
                        copy_img(T, c, 0)
                        copy_t(T + 3, 1)
                        if within(edge, 0, NCH, 1) and edge != 0:
                            normalise(i * 12 + 13 + h + par, 1 - par)
                        copy_img(T + 1, c, 1)
                        if within(edge, 0, NCH, 1) and edge != 0:
                            high_part(i * 16 + c + (NCH + 1), 1 - par, patches=True)
                        copy_img(T + 2, c, 2)
                        copy_img(T + 3, c, 3)
                    if edge == 0:
                        for k in range(KB):
                            first_tap(c, k)
                steps(act, NCH + 2, 2, NCH - 2, part_c)

        @block.vector
        def _(dve):
            dve.wait_ge(s_init, 1)
            nc.vector.tensor_copy(ones_r[:], ones_f[:])
            nc.vector.memset(bn_x1[:], 1.0)
            nc.vector.memset(gvar[:], 1.0)
            dve.wait_ge(s_raw, 16)
            count = [0]

            def link(ins):
                count[0] += 1
                ins.then_inc(s_setup_p, 1)
                dve.wait_ge(s_setup_p, count[0])

            def split(hi, lo, raw, scale):
                link(nc.vector.tensor_scalar(hi, raw, scale, None, ALU.mult))
                return nc.vector.scalar_tensor_tensor(lo, raw, scale, hi.bitcast(fp32), ALU.mult, ALU.subtract)

            for a, b, scale in SPLIT:
                ins = split(w_hi[:, :, a:b], w_lo[:, :, a:b], w_raw[:, :, a:b], scale)
            ins.then_inc(s_setup_v, 1)

            def x_stats(h, par, c):
                dve.wait_ge(s_xa[par], h * 16)
                for k in range(KB):
                    ins = nc.vector.bn_stats(bn_x[:, k, ds(c, 1), :].rearrange("p c s -> p (c s)"), xa[:, par, k])
                ins.then_inc(s_stat, 1)

            for c in range(NCH):
                x_stats(c // 2 + 1, c % 2, c)

            dve.wait_ge(s_raw, 48)
            link(split(win_hi[:], win_lo[:], w_raw[:, :, 0:C], 1.0))
            dve.wait_ge(s_cst, NCST * 16)
            for a, b, scale in SPLIT[:4]:
                hi, raw = qkbias[:, a:b], w_raw[:, 0, C + a:C + b]
                tmp = w_raw[:, 1, C + a:C + b]
                link(split(hi, tmp, raw, scale))
                link(nc.vector.tensor_scalar(tmp, tmp, t_rowpick[:, 1:2], None, ALU.mult))
                ins = nc.vector.scalar_tensor_tensor(hi, hi.bitcast(fp32), t_rowpick[:, 0:1], tmp, ALU.mult, ALU.add)
            ins.then_inc(s_setup_v, 1)
            dve.wait_ge(s_setup_a, 1)
            nc.vector.tensor_copy(fsel[:], bank[0][:, 0:C]).then_inc(s_setup_v, 1)

            def group_norm(f):
                g = f * 11

                def nxt(ins, k):
                    ins.then_inc(s_gs, 1)
                    dve.wait_ge(s_gs, g + k)

                dve.wait_ge(s_stat, f * NCH + NCH)
                dve.wait_ge(s_x1s, f * NCH + 2)
                dve.sem_inc(s_past, 1)
                for s, bn in enumerate((bn_x, bn_x1)):
                    for k in range(KB):
                        ins = nc.vector.bn_aggr(mv[:, s, k], bn[:, k].rearrange("p c s -> p (c s)"))
                nxt(ins, 1)
                dve.wait_ge(s_gp, f * 2 + 1)
                pm = bank[7][:, 0:2 * KB].rearrange("p (m s) -> p s m", s=2)
                nc.vector.tensor_copy(gmean[:, :, :], pm)
                nxt(nc.vector.tensor_tensor(dev[:, :, :], mv[:, :, :, 0], pm, ALU.subtract), 2)
                nxt(nc.vector.tensor_tensor(newt[:, :, :], dev[:, :, :], dev[:, :, :], ALU.mult), 3)
                nxt(nc.vector.tensor_tensor(dev[:, :, :], newt[:, :, :], mv[:, :, :, 1], ALU.add), 4)
                dve.wait_ge(s_gp, f * 2 + 2)
                nxt(nc.vector.tensor_scalar(gvar[:, :, :], pm, GN_EPS, None, ALU.add), 5)
                dve.wait_ge(s_ga, f + 1)
                nxt(nc.vector.reciprocal(rstd[:, :, :], gstd[:, :, :]), 6)
                nxt(nc.vector.tensor_tensor(newt[:, :, :], rstd[:, :, :], rstd[:, :, :], ALU.mult), 7)
                nxt(nc.vector.tensor_tensor(newt[:, :, :], newt[:, :, :], gvar[:, :, :], ALU.mult), 8)
                nxt(nc.vector.tensor_scalar(newt[:, :, :], newt[:, :, :], -0.5, 1.5, ALU.mult, ALU.add), 9)
                nxt(nc.vector.tensor_tensor(rstd[:, :, :], rstd[:, :, :], newt[:, :, :], ALU.mult), 10)
                nxt(nc.vector.scalar_tensor_tensor(shift[:, :, :], gmean[:, :, :], -1.0, rstd[:, :, :], ALU.mult, ALU.mult), 11)

            group_norm(0)

            def normalise(s, loads, par):
                dve.wait_ge(s_xa[par], loads * 16)
                for k in range(KB):
                    nc.vector.tensor_scalar(xa[:, par, k], xa[:, par, k], gmean[:, s, k:k + 1],
                                            rstd[:, s, k:k + 1], ALU.subtract, ALU.mult).then_inc(s_nrm, 1)

            def rope(T, tile, p2):
                wide = [P, 2, ROT, 2]
                dve.wait_ge(s_elu, T + 1)
                tabs = [(t_cosh[:, ds(tile, 1), :].rearrange("p a f -> p (a f)"),
                         t_sinh[:, ds(tile, 1), :].rearrange("p a f -> p (a f)")),
                        (t_csw[:, 0, :], t_csw[:, 1, :])]
                for b in range(2):
                    dve.wait_ge(s_qkv, T * 3 + (b + 1))
                    src = bank[3 * p2 + b][:, 0:C].rearrange("p (s f r) -> p s f r", s=2, r=2)
                    for dst, tab in zip((t1, t2), tabs[b]):
                        ins = nc.vector.tensor_tensor(dst[:, p2, b].rearrange("p s (f r) -> p s f r", r=2), src,
                                                      tab.unsqueeze(1).unsqueeze(3).to_broadcast(wide), ALU.mult)
                ins.then_inc(s_rope, 1)

            def elu(T, tile, p2):
                dve.wait_ge(s_exp, T * 2 + 2)
                dve.wait_ge(s_kv, T + 1)
                qdst = q_all[:, ds(tile, 1), :].rearrange("p a (b f) -> p (a b) f", b=2)
                for s, dst in enumerate((qdst, kt[:, p2].rearrange("p (b f) -> p b f", b=2))):
                    ins = nc.vector.scalar_tensor_tensor(dst, t2[:, p2, :, s], 1.0, t1[:, p2, :, s], ALU.min, ALU.add)
                ins.then_inc(s_elu, 1)

            normalise(0, 5, 0)
            rope(0, 0, 0)
            with dve.Fori(0, images) as i:

                def part_a(c, h, edge, par):
                    T = (i * 8 + c) * 4
                    if within(edge, 0, NCH, 1):
                        normalise(0, i * 12 + 5 + h + par, 1 - par)
                    for j in range(TPC):
                        if j < TPC - 1 or within(edge, 0, NCH, 1):
                            rope(T + j + 1, c * 4 + (j + 1), (j + 1) % 2)
                        elu(T + j, c * 4 + j, j % 2)
                steps(dve, NCH, 0, NCH - 2, part_a)

                kvp = bank[KVB][:, 0:KB * (P + 1)].rearrange("p (k n) -> p k n", k=KB)
                dve.wait_ge(s_kv, i * NT + (NT + 2))
                nc.vector.tensor_copy(ksum[:, :], kvp[:, :, P]).then_inc(s_kd, 1)
                dve.wait_ge(s_kd, i * 4 + 1)
                for j in range(KB):
                    ins = nc.vector.tensor_scalar(kdiag[:, j], ident, ksum[:, j:j + 1], None, ALU.mult)
                ins.then_inc(s_kd, 1)
                for j in range(KB):
                    ins = nc.vector.scalar_tensor_tensor(kvfix[:, j], bv_bc[:, j * P:(j + 1) * P], ksum[:, j:j + 1],
                                                         kvp[:, j, 0:P], ALU.mult, ALU.add)
                ins.then_inc(s_kd, 1)
                dve.wait_ge(s_kd, i * 4 + 3)
                nc.vector.tensor_tensor(kvfix[:, :, :], kvfix[:, :, :], headmask.unsqueeze(1).to_broadcast([P, KB, P]),
                                        ALU.mult).then_inc(s_kd, 1)

                def divide_q(c, par):
                    n = i * 8 + c
                    by_head = qn[:, par].rearrange("p t (h d) -> p (t h) d", d=HD)
                    dve.wait_ge(s_prod, n + 1)
                    dve.wait_ge(s_qn, n + 1)
                    nc.vector.tensor_reduce(nrm[:, :], by_head, AX.X, ALU.add).then_inc(s_nd, 1)
                    dve.wait_ge(s_nd, n * 3 + 1)
                    nc.vector.tensor_scalar(nrm[:, :], nrm[:, :], NORM_EPS, None, ALU.add).then_inc(s_nd, 1)
                    dve.wait_ge(s_nd, n * 3 + 2)
                    nc.vector.reciprocal(nrm[:, :], nrm[:, :]).then_inc(s_nd, 1)
                    dve.wait_ge(s_nd, n * 3 + 3)
                    nc.vector.tensor_tensor(by_head, q_all[:, ds(c * 4, 4), :].rearrange("p t (h d) -> p (t h) d", d=HD),
                                            nrm[:, :].unsqueeze(2).to_broadcast([P, TPC * HEADS, HD]), ALU.mult)\
                        .then_inc(s_qn, 1)

                def residual(r, loads, par, bias, tail=False):
                    dve.wait_ge(s_xr[par], loads * 16)
                    for m in range(KB):
                        dve.wait_ge(s_out, r * 3 + (m + 7))
                        ps = bank[2 + 3 * par + m if bias else out_bank(m, tail)][:, :]
                        if bias:
                            ins = nc.vector.scalar_tensor_tensor(xr[:, par, m], ps, bfc_c[:, m:m + 1], xr[:, par, m],
                                                                 ALU.add, ALU.add)
                        else:
                            ins = nc.vector.tensor_tensor(xr[:, par, m], ps, xr[:, par, m], ALU.add)
                        ins.then_inc(s_res, 1)

                divide_q(0, 0)

                def part_b(c, h, edge, par):
                    if within(edge, 0, NCH, 1):
                        divide_q(c + 1, 1 - par)
                    if within(edge, 0, NCH, -1):
                        residual(i * 16 + c - 1, i * 8 + h + par, 1 - par, True)
                    if within(edge, 0, NCH):
                        x_stats(i * 12 + 9 + h, par, c)
                    if within(edge, 0, NCH, -1):
                        dve.wait_ge(s_res, (i * 16 + c) * 3 + 6)
                        for k in range(KB):
                            ins = nc.vector.bn_stats(bn_x1[:, k, ds(c - 1, 1), :].rearrange("p c s -> p (c s)"),
                                                     xr[:, 1 - par, k])
                        ins.then_inc(s_x1s, 1)
                steps(dve, NCH + 1, 1, NCH - 1, part_b)
                group_norm(i + 1)

                def times_filter(T, p2):
                    dve.wait_ge(s_dft, T + 3)
                    dve.wait_ge(s_inv, T + 1)
                    nc.vector.tensor_tensor(gb[:, p2], bank[2 + p2][:, 0:C], fsel[:, :], ALU.mult).then_inc(s_f, 1)

                ORDER = [(dy, dx) for dy in (-1, 0, 1) for dx in (-1, 0, 1)]

                def depthwise(c, q0, q1):
                    n = i * 8 + c
                    for q in range(q0, q1):
                        (dy, dx), k = ORDER[1 + q // KB], q % KB
                        src = filt_img[:, k, ds(c * ROWS + (1 + dy), ROWS), 1 + dx:1 + dx + W]
                        tap = wdw[:, k, 1 + q // KB:2 + q // KB]
                        dst = acc[:, k].rearrange("p (r s) -> p r s", s=W)
                        if q < KB:
                            dve.wait_ge(s_tap, n * 3 + (k + 1))
                        else:
                            dve.wait_ge(s_dw, n * 24 + (q - KB + 1))
                        nc.vector.scalar_tensor_tensor(dst, src, tap, dst, ALU.mult, ALU.add).then_inc(s_dw, 1)

                def gate(c, m):
                    n = i * 8 + c
                    dve.wait_ge(s_dw, n * 24 + 24)
                    dve.wait_ge(s_gel, n * 2 + (m + 3))
                    a, b = (0, 1) if m == 0 else (HD, 2)
                    nc.vector.tensor_tensor(gel[a:P, m], gel[a:P, m], acc[a:P, b], ALU.mult).then_inc(s_gate, 1)

                for u in range(2):
                    normalise(1, i * 12 + 13, u)
                dve.wait_ge(s_brd, i + 1)

                def part_c(c, h, edge, par):
                    T = (i * 8 + c) * 4
                    tile, conv = within(edge, 0, NCH), within(edge, 0, NCH, -1)
                    parts = (0, 6, 9, 12, 15) if edge == 1 else (0, 5, 10, 15, 15)
                    if tile:
                        times_filter(T, 0)
                    if within(edge, 0, NCH, -2):
                        gate(c - 2, 0)
                        gate(c - 2, 1)
                    if edge == NCH:
                        normalise(0, i * 12 + 17, 0)
                    if conv and edge != 1:
                        depthwise(c - 1, parts[0], parts[1])
                    if tile:
                        times_filter(T + 1, 1)
                    if conv:
                        depthwise(c - 1, parts[1], parts[2])
                    if tile:
                        times_filter(T + 2, 0)
                    if conv:
                        depthwise(c - 1, parts[2], parts[3])
                    if tile:
                        times_filter(T + 3, 1)
                    if conv:
                        depthwise(c - 1, parts[3], parts[4])
                    if edge == 0:
                        depthwise(c, 0, 6)
                    if edge == NCH + 1:
                        dve.wait_ge(s_gate, i * 16 + 18)
                        rope((i + 1) * NT, 0, 0)
                    if within(edge, 0, NCH, -2):
                        residual(i * 16 + c + (NCH - 2), i * 8 + 4 + h, par, False, tail=(edge == NCH + 1))
                    if conv:
                        if tile:
                            dve.wait_ge(s_img, T + 6)
                        depthwise(c - 1, 15, 24)
                steps(dve, NCH + 2, 2, NCH - 2, part_c)

        @block.tensor
        def _(pe):
            pe.wait_ge(s_init, 1)
            pe.wait_ge(s_cst, NCST * 16)
            nc.tensor.matmul(bank[0][:, 0:C], sel, fsel[:, :], start=True, stop=True).then_inc(s_setup_a, 1)

            def group_avg(f):
                for step, (wait, src) in enumerate(((1, lambda k: mv[:, :, k, 0]), (4, lambda k: dev[:, :, k]))):
                    pe.wait_ge(s_gs, f * 11 + wait)
                    for m in range(KB):
                        ks = [k for k, mm in GBLOCKS if mm == m]
                        for k in ks:
                            ins = nc.tensor.matmul(bank[7][:, 2 * m:2 * m + 2], t_gavg[:, GBLOCKS.index((k, m)), :], src(k),
                                                   start=(k == ks[0]), stop=(k == ks[-1]))
                    ins.then_inc(s_gp, 1)

            group_avg(0)
            pe.wait_ge(s_setup_v, 3)

            def split_product(dst, hi, lo, whi, wlo, m=None, first=True):
                for k in range(KB):
                    if m is not None:
                        pe.wait_ge(s_hi, m * 3 + (k + 1))
                    nc.tensor.matmul(dst, hi(k), whi(k), start=first and k == 0, stop=False)
                    nc.tensor.matmul(dst, hi(k), wlo(k), start=False, stop=False)
                for k in range(KB):
                    if m is not None:
                        pe.wait_ge(s_lo, m * 3 + (k + 7))
                    ins = nc.tensor.matmul(dst, lo(k), whi(k), start=False, stop=(k == KB - 1))
                return ins

            def project(T, m, par, j):
                p2 = j % 2
                pe.wait_ge(s_rope, T + 1)
                pe.wait_ge(s_v, T + 1)
                tok = slice(j * P, (j + 1) * P)
                for b in range(3):
                    dst = bank[3 * p2 + b][:, 0:C]
                    cols = slice(b * C, (b + 1) * C)
                    if b < 2:
                        nc.tensor.matmul(dst, ones_r[:, :], qkbias[:, cols], start=True, stop=False)
                    ins = split_product(dst, lambda k: x_hi[:, par, k, tok], lambda k: x_lo[:, par, k, tok],
                                        lambda k: w_hi[:, k, cols], lambda k: w_lo[:, k, cols],
                                        m if j == 0 and b == 0 else None, first=(b == 2))
                    ins.then_inc(s_qkv, 1)

            def add_kv(T, j, first=False, last=False, frees=False):
                pe.wait_ge(s_elu, T + 3)
                pe.wait_ge(s_v, T + 3)
                p2 = j % 2
                for k in range(KB):
                    ins = nc.tensor.matmul(bank[KVB][:, k * (P + 1):(k + 1) * (P + 1)], kt[:, p2, k * P:(k + 1) * P],
                                           vt[:, p2, k, :], start=(first and k == 0), stop=last, skip_group_check=True)
                    if frees and k == 0:
                        ins.then_inc(s_xfree, 1)
                ins.then_inc(s_kv, 1)

            for j in range(2):
                project(j, 0, 0, j)
            with pe.Fori(0, images) as i:
                pe.wait_ge(s_res, i * 48 + 6)

                def part_a(c, h, edge, par):
                    T = (i * 8 + c) * 4
                    first = edge == 0
                    m = i * 16 + c
                    project(T + 2, m, par, 2)
                    add_kv(T, 0, first=first)
                    project(T + 3, m, par, 3)
                    add_kv(T + 1, 1, frees=True)
                    if within(edge, 0, NCH, 1):
                        project(T + 4, m + 1, 1 - par, 0)
                    add_kv(T + 2, 2)
                    if within(edge, 0, NCH, 1):
                        project(T + 5, m + 1, 1 - par, 1)
                    add_kv(T + 3, 3, last=(edge == NCH - 1))

                steps(pe, NCH, 2, NCH - 2, part_a)

                pe.wait_ge(s_kd, i * 4 + 2)
                nc.tensor.matmul(bank[0][:, 0:C], ones_f[:, :], kdiag[:, :, :], start=True, stop=True).then_inc(s_kp, 1)
                pe.wait_ge(s_kd, i * 4 + 4)
                for j in range(KB):
                    ins = nc.tensor.transpose(bank[1][:, j * P:(j + 1) * P], kvfix[:, j], ident)
                ins.then_inc(s_kp, 1)
                pe.wait_ge(s_ka, i * 3 + 2)
                for j in range(KB):
                    nc.tensor.matmul(bank[2 + j][:, 0:C], kv_t[:, j], wfc[:, j], start=True, stop=True).then_inc(s_kp, 1)
                pe.wait_ge(s_ka, i * 3 + 3)

                def transpose_q(c, par):
                    n = i * 8 + c
                    pe.wait_ge(s_qn, n + 2)
                    for j in range(KB):
                        pe.wait_ge(s_qt, n * 3 + (j + 1))
                        for u in range(TPC):
                            ins = nc.tensor.transpose(bank[(par + j) % 2][:, u * P:(u + 1) * P],
                                                      qn[:, par, u, j * P:(j + 1) * P], ident)
                        ins.then_inc(s_tp, 1)

                transpose_q(0, 0)

                def part_b(c, h, edge, par):
                    r = (i * 16 + c) * 3
                    for m in range(KB):
                        if m == KB - 1 and within(edge, 0, NCH, 1):
                            transpose_q(c + 1, 1 - par)
                        pe.wait_ge(s_res, r + (m + 1))
                        for j in range(KB):
                            if m == 0:
                                pe.wait_ge(s_qt, (i * 8 + c) * 3 + (j + 3))
                            ins = nc.tensor.matmul(bank[2 + 3 * par + m][:, :], mout[:, j, m * P:(m + 1) * P],
                                                   qt[:, par, j], start=(j == 0), stop=(j == KB - 1))
                        ins.then_inc(s_out, 1)
                steps(pe, NCH, 0, NCH - 2, part_b)
                group_avg(i + 1)

                pe.wait_ge(s_res, i * 48 + (3 * NCH + 6))

                def t_tile(T, m, par, j):
                    p2 = j % 2
                    pe.wait_ge(s_t, T + 1)
                    pix = slice(j * P, (j + 1) * P)
                    split_product(bank[p2][:, 0:C], lambda k: x_hi[:, par, k, pix], lambda k: x_lo[:, par, k, pix],
                                  lambda k: win_hi[:, k], lambda k: win_lo[:, k], m if j == 0 else None).then_inc(s_tm, 1)

                def dft_tile(T, j):
                    p2 = j % 2
                    pe.wait_ge(s_t, T + 3)
                    pe.wait_ge(s_f, T + 1)
                    nc.tensor.matmul(bank[2 + p2][:, 0:C], phi, tb[:, p2], start=True, stop=True).then_inc(s_dft, 1)

                def inverse_tile(T, j, frees=False):
                    p2 = j % 2
                    pe.wait_ge(s_f, T + 3)
                    pe.wait_ge(s_img, T + 2)
                    for k in range(KB):
                        ins = nc.tensor.matmul(bank[4][:, k * P:(k + 1) * P], gb[:, p2, k * P:(k + 1) * P], phi_t,
                                               start=True, stop=True)
                        if frees and k == 0:
                            ins.then_inc(s_xfree, 1)
                    ins.then_inc(s_inv, 1)

                def out_block(c, m, tail=False):
                    pe.wait_ge(s_gate, (i * 8 + c) * 2 + 4)
                    pe.wait_ge(s_res, (i * 16 + c + NCH) * 3 + (m + (5 if tail else 4)))
                    dst = bank[out_bank(m, tail)][:, :]
                    nc.tensor.matmul(dst, wout[:, 0, m * P:(m + 1) * P], gel[:, 0], start=True, stop=False)
                    nc.tensor.matmul(dst, wout[HD:P, 1, m * P:(m + 1) * P], gel[HD:P, 1], start=False, stop=True)\
                        .then_inc(s_out, 1)

                def part_c(c, h, edge, par):
                    T = (i * 8 + c) * 4
                    m = i * 16 + c + NCH
                    tile, prod = within(edge, 0, NCH), within(edge, 0, NCH, -2)
                    if tile:
                        t_tile(T, m, par, 0)
                        t_tile(T + 1, m, par, 1)
                        dft_tile(T, 0)
                        t_tile(T + 2, m, par, 2)
                        dft_tile(T + 1, 1)
                        inverse_tile(T, 0)
                    if edge == NCH + 1:
                        pe.wait_ge(s_res, i * 48 + (3 * (2 * NCH - 1) + 6))
                        pe.wait_ge(s_img, (i + 1) * NT + 2)
                        pe.wait_ge(s_f, (i + 1) * NT + 2)
                        pe.wait_ge(s_t, (i + 1) * NT + 2)
                        for j in range(2):
                            project((i + 1) * NT + j, (i + 1) * 16, 0, j)
                    if prod:
                        out_block(c - 2, 0, edge == NCH + 1)
                    if tile:
                        t_tile(T + 3, m, par, 3)
                        dft_tile(T + 2, 2)
                        inverse_tile(T + 1, 1, frees=True)
                    if prod:
                        out_block(c - 2, 1, edge == NCH + 1)
                    if tile:
                        dft_tile(T + 3, 3)
                        inverse_tile(T + 2, 2)
                        inverse_tile(T + 3, 3)
                    if prod:
                        out_block(c - 2, 2, edge == NCH + 1)
                steps(pe, NCH + 2, 2, NCH, part_c)


def kernel(x, L0_conv_Wq, L0_conv_bq, L0_conv_Wk, L0_conv_bk, L0_conv_Wv, L0_conv_bv, L0_conv_Wfc, L0_conv_bfc,
           L1_conv_fft_filter, L1_conv_w_in, L1_conv_w_dw, L1_conv_w_out):
    import concourse.bacc as bacc
    from concourse.bass_utils import run_bass_kernel_spmd

    a = np.asarray
    images = x.shape[0]
    wq, wk, wv = a(L0_conv_Wq).T, a(L0_conv_Wk).T, a(L0_conv_Wv).T
    bq, bk = a(L0_conv_bq), a(L0_conv_bk)
    half = C // 2
    order = np.concatenate([np.arange(P), half + np.arange(P), np.arange(P, half), half + np.arange(P, half)])
    wo = a(L1_conv_w_out).T
    wout = np.zeros((P, 2, C), wo.dtype)
    wout[:, 0] = wo[:P]
    wout[HD:, 1] = wo[P:]
    arrays = {
        "x": a(x).reshape(images, C, NTOK),
        "wqkv_t": np.concatenate([wq[:, :HALF], wk[:, :HALF], wq[:, HALF:], wk[:, HALF:], wv], axis=1),
        "bqk": np.concatenate([bq[:HALF], bk[:HALF], bq[HALF:], bk[HALF:]])[None],
        "bv": a(L0_conv_bv)[None],
        "wfc_t": a(L0_conv_Wfc).T,
        "bfc": a(L0_conv_bfc).reshape(KB, P).T,
        "filt": a(L1_conv_fft_filter)[order].reshape(C, -1).T,
        "w_in_t": a(L1_conv_w_in)[order].T,
        "w_dw": a(L1_conv_w_dw)[order].reshape(KB, P, TAPS).transpose(1, 0, 2),
        "w_out_t": wout,
    }
    arrays.update(constants())
    arrays = {k: np.ascontiguousarray(v) for k, v in arrays.items()}
    nc = bacc.Bacc("TRN2", target_bir_lowering=False, num_devices=1)
    aps = {k: nc.dram_tensor(k, v.shape, mybir.dt.from_np(v.dtype), kind="ExternalInput").ap() for k, v in arrays.items()}
    out = nc.dram_tensor("out", (images, C, NTOK), mybir.dt.float32, kind="ExternalOutput").ap()
    build_program(nc, **aps, out=out, images=images)
    r = run_bass_kernel_spmd(nc, [arrays], core_ids=[0])
    return r.results[0]["out"].reshape(images, C, H, W)
```

```python
import math

import numpy as np
import concourse.bass as bass
from concourse import mybir
from contextlib import ExitStack

B, C, H, W = 8, 384, 64, 64
NTOK = H * W
P = 128
KB = C // P
CHUNK = 512
NCH = NTOK // CHUNK
ROWS = CHUNK // W
TPC = CHUNK // P
NT = NCH * TPC
HEADS, HD = 6, 64
HALF = C // 2
ROT = HALF // 2
GROUP = C // 32
PATCH = 8
HP, WP = H + 2, W + 2
TAPS = 9
PE_TAPS, PE_BLOCKS = 2, 2
FIRST_TAP = [PE_TAPS if k < PE_BLOCKS else 1 for k in range(KB)]
DW_STEPS = (sorted(((q, k) for k in range(KB) for q in range(FIRST_TAP[k], 6)), key=lambda s: (s[0] - FIRST_TAP[s[1]], s[1]))
            + [(q, k) for q in range(6, TAPS) for k in range(KB)])
ND = len(DW_STEPS)
GN_EPS = 1e-5
NORM_EPS = 1e-6
THETA = 10000.0
GBLOCKS = [(k, m) for m in range(KB) for k in range(KB) if abs(k - m) <= 1]


def rotary_tables():
    inv = (np.float32(1.0) / np.float32(THETA) ** (np.arange(0, HALF, 2, dtype=np.float32) / np.float32(HALF))).astype(np.float32)
    part = np.arange(P)
    rows = (np.arange(NT)[None, :] * (P // W) + part[:, None] // W).astype(np.float32)
    cols = (part % W).astype(np.float32)
    ang_h = (rows[:, :, None] * inv).astype(np.float32).astype(np.float64)
    ang_w = (cols[:, None] * inv).astype(np.float32).astype(np.float64)
    nf = ROT // 2

    def source_sin(ang):
        s = np.sin(ang)
        return np.concatenate([s[..., nf:], -s[..., :nf]], axis=-1)

    f32 = np.float32
    return (np.cos(ang_h).astype(f32), source_sin(ang_h).astype(f32),
            np.cos(ang_w).astype(f32), source_sin(ang_w).astype(f32))


def patch_basis():
    n = PATCH
    r, s = np.meshgrid(np.arange(n), np.arange(n), indexing="ij")
    funcs, picks = [], []
    for u in range(n):
        for v in range(n // 2 + 1):
            if v in (0, n // 2):
                if u > n // 2:
                    continue
                pick = np.zeros((n, n // 2 + 1))
                pick[u, v] += 0.5
                pick[(-u) % n, v] += 0.5
            else:
                pick = np.zeros((n, n // 2 + 1))
                pick[u, v] = 1.0
            ang = 2 * np.pi * ((u * r + v * s) % n) / n
            for f in (np.cos(ang), np.sin(ang)):
                norm = np.sqrt((f ** 2).sum())
                if norm > 1e-6:
                    funcs.append(f / norm)
                    picks.append(pick.ravel())
    funcs, picks = np.array(funcs), np.array(picks)
    assert len(funcs) == n * n
    phi = np.zeros((P, P))
    sel = np.zeros((P, P))
    for pp in range(2):
        for k in range(n * n):
            for rr in range(n):
                phi[rr * 16 + pp * 8:rr * 16 + pp * 8 + 8, pp * 64 + k] = funcs[k][rr]
            sel[:n * (n // 2 + 1), pp * 64 + k] = picks[k]
    return phi.astype(np.float32), sel.astype(np.float32)


def constants():
    cos_h, sin_h, cos_w, sin_w = rotary_tables()
    phi, sel = patch_basis()
    g = np.kron(np.eye(C // GROUP), np.full((GROUP, GROUP), 1.0 / GROUP)).astype(np.float32)
    gavg = np.stack([g[k * P:(k + 1) * P, m * P:(m + 1) * P] for k, m in GBLOCKS], axis=1)
    rowpick = np.zeros((P, 2), np.float32)
    rowpick[0, 0] = 1.0
    rowpick[1, 1] = 1.0
    return {
        "cos_h": cos_h, "sin_h": sin_h,
        "cs_w": np.stack([cos_w, sin_w], axis=1),
        "mats": np.stack([np.eye(P, dtype=np.float32),
                          np.kron(np.eye(2), np.ones((HD, HD))).astype(np.float32),
                          phi, np.ascontiguousarray(phi.T), sel], axis=1),
        "gavg": np.ascontiguousarray(gavg),
        "rowpick": rowpick,
    }


def build_program(nc, x, wqkv_t, bqk, bv, wfc_t, bfc, filt, w_in_t, w_dw, w_out_t,
                  cos_h, sin_h, cs_w, mats, gavg, rowpick, out, images=B):
    fp32, fp32r = mybir.dt.float32, mybir.dt.float32r
    ALU, ACT, AX = mybir.AluOpType, mybir.ActivationFunctionType, mybir.AxisListType
    ds = bass.ds

    x_v = x.rearrange("b (k p) (c n) -> b p k c n", p=P, n=CHUNK)
    out_v = out.rearrange("b (k p) (c n) -> b p k c n", p=P, n=CHUNK)
    x1_dram = nc.dram_tensor("x1_scratch", (images, C, NTOK), fp32, kind="Internal").ap()
    x1_v = x1_dram.rearrange("b (k p) (c n) -> b p k c n", p=P, n=CHUNK)

    ctx = ExitStack()
    with ctx:
        def sb(name, shape, dt=fp32):
            return ctx.enter_context(nc.sbuf_tensor(name, shape, dt))

        def sem(name):
            return ctx.enter_context(nc.semaphore(name))

        t_cosh = sb("t_cosh", [P, NT, ROT])
        t_sinh = sb("t_sinh", [P, NT, ROT])
        t_csw = sb("t_csw", [P, 2, ROT])
        t_mats = sb("t_mats", [P, 5, P])
        ident, headmask, phi, phi_t, sel = (t_mats[:, j, :] for j in range(5))
        t_gavg = sb("t_gavg", [P, len(GBLOCKS), P])
        t_rowpick = sb("t_rowpick", [P, 2])
        ones_f = sb("ones_f", [P, P])
        ones_r = sb("ones_r", [P, P], fp32r)
        w_hi = sb("w_hi", [P, KB, 3 * C], fp32r)
        w_lo = sb("w_lo", [P, KB, 3 * C], fp32r)
        qkbias = sb("qkbias", [P, 2 * C], fp32r)
        bv_bc = sb("bv_bc", [P, C])
        wfc = sb("wfc", [P, KB, C])
        bfc_c = sb("bfc_c", [P, KB])
        win_hi = sb("win_hi", [P, KB, C], fp32r)
        win_lo = sb("win_lo", [P, KB, C], fp32r)
        wdw = sb("wdw", [P, KB, TAPS])
        wout = sb("wout", [P, 2, C])
        fsel = sb("fsel", [P, C])
        tapdiag = sb("tapdiag", [P, PE_BLOCKS, PE_TAPS, P])
        bn_x = sb("bn_x", [P, KB, NCH, 6])
        bn_x1 = sb("bn_x1", [P, KB, NCH, 6])
        mv = sb("mv", [P, 2, KB, 2])
        dev = sb("dev", [P, 2, KB])
        gmean = sb("gmean", [P, 2, KB])
        gvar = sb("gvar", [P, 2, KB])
        gstd = sb("gstd", [P, 2, KB])
        rstd = sb("rstd", [P, 2, KB])
        newt = sb("newt", [P, 2, KB])
        shift = sb("shift", [P, 2, KB])
        counted = sb("counted", [P, 32])
        ksum = sb("ksum", [P, KB])
        nrm = sb("nrm", [P, TPC * HEADS])
        big = sb("big", [P, KB * HP * WP])
        q_all = big[:, 0:NT * C].rearrange("p (t c) -> p t c", c=C)
        first_x = big[:, 0:KB * NTOK].rearrange("p (c k n) -> p c k n", c=NCH, k=KB)
        filt_img = big[:, :].rearrange("p (k y z) -> p k y z", k=KB, z=WP)
        xr = sb("xr", [P, 2, KB, CHUNK])

        def overlay(*variants):
            made = []
            for variant in variants[:-1]:
                with ExitStack() as inner:
                    made.append([inner.enter_context(nc.sbuf_tensor(n, s, d)) for n, s, d in variant])
            made.append([sb(n, s, d) for n, s, d in variants[-1]])
            return made

        (kbc, mout_hi, mout_lo, qt_hi), (x_hi, x_lo) = overlay(
            [("kbc", [P, C], fp32), ("mout_hi", [P, KB, C], fp32r), ("mout_lo", [P, KB, C], fp32r),
             ("qt_hi", [P, 2, KB, CHUNK], fp32r)],
            [("x_hi", [P, 2, KB, CHUNK], fp32r), ("x_lo", [P, 2, KB, CHUNK], fp32r)])
        (kvfix, kdiag, kv_t), (qt_lo, ), (xa, ) = overlay(
            [("kvfix", [P, KB, P], fp32), ("kdiag", [P, KB, P], fp32), ("kv_t", [P, KB, P], fp32)],
            [("qt_lo", [P, 2, KB, CHUNK], fp32r)],
            [("xa", [P, 2, KB, CHUNK], fp32)])
        (w_raw, ), (qn, ), (t1, t2, kt), (tb, gb, acc, gel) = overlay(
            [("w_raw", [P, KB, 3 * C], fp32)],
            [("qn", [P, 2, TPC, C], fp32)],
            [("t1", [P, 2, 2, 2, HALF], fp32), ("t2", [P, 2, 2, 2, HALF], fp32), ("kt", [P, 2, C], fp32)],
            [("tb", [P, 2, C], fp32), ("gb", [P, 2, C], fp32), ("acc", [P, KB, CHUNK], fp32),
             ("gel", [P, 2, CHUNK], fp32)])
        vt = sb("vt", [P, 2, KB, P + 1])

        bank = [ctx.enter_context(nc.psum_tensor(f"bank{j}", [P, 512], fp32)) for j in range(8)]
        KVB = 6

        s_init = sem("s_init")
        s_cst = sem("s_cst")
        s_tab = sem("s_tab")
        s_late = sem("s_late")
        s_first = [sem(f"s_first{c}") for c in range(NCH)]
        s_raw = sem("s_raw")
        s_filter = sem("s_filter")
        s_split = sem("s_split")
        s_link = sem("s_link")
        s_xa = [sem(f"s_xa{j}") for j in range(2)]
        s_xr = [sem(f"s_xr{j}") for j in range(2)]
        s_st = [sem(f"s_st{j}") for j in range(2)]
        s_stat = sem("s_stat")
        s_x1s = sem("s_x1s")
        s_nrm = sem("s_nrm")
        s_hi = sem("s_hi")
        s_lo = sem("s_lo")
        s_xfree = sem("s_xfree")
        s_qkv = sem("s_qkv")
        s_rope = sem("s_rope")
        s_add = sem("s_add")
        s_exp = sem("s_exp")
        s_elu = sem("s_elu")
        s_v = sem("s_v")
        s_kv = sem("s_kv")
        s_kd = sem("s_kd")
        s_kp = sem("s_kp")
        s_ka = sem("s_ka")
        s_prod = sem("s_prod")
        s_nd = sem("s_nd")
        s_qn = sem("s_qn")
        s_qnp = sem("s_qnp")
        s_mlo = sem("s_mlo")
        s_tp = sem("s_tp")
        s_qt = sem("s_qt")
        s_ql = sem("s_ql")
        s_out = sem("s_out")
        s_res = sem("s_res")
        s_gs = sem("s_gs")
        s_gp = sem("s_gp")
        s_ga = sem("s_ga")
        s_tm = sem("s_tm")
        s_t = sem("s_t")
        s_dft = sem("s_dft")
        s_f = sem("s_f")
        s_inv = sem("s_inv")
        s_img = sem("s_img")
        s_brd = sem("s_brd")
        s_tap = sem("s_tap")
        s_ptap = sem("s_ptap")
        s_dw = sem("s_dw")
        s_gel = sem("s_gel")
        s_gate = sem("s_gate")

        s_past = sem("s_past")

        AHEAD = {s_lo: 6, s_xfree: 2, s_rope: 2, s_v: 2, s_kv: 2, s_tp: 6, s_ql: 2, s_qnp: 1, s_res: 6, s_t: 2,
                 s_dft: 2, s_f: 2, s_inv: 2, s_img: 2, s_x1s: 2, s_out: 6, s_elu: 2, s_qn: 1,
                 s_gate: 2, s_gel: 2, s_st[0]: 16, s_st[1]: 16}

        def steps(eng, total, lo, hi, body):
            for c in range(lo):
                body(c, c // 2, c, c % 2)
            with eng.Fori(0, (hi - lo) // 2) as k:
                for u in range(2):
                    body(k * 2 + (lo + u), k + (lo + u) // 2, None, (lo + u) % 2)
            for c in range(hi, total):
                body(c, c // 2, c, c % 2)

        def within(edge, a, b, off=0):
            return edge is None or a <= edge + off < b

        def chunk_of(view, i, c):
            return view[ds(i, 1), :, :, ds(c, 1), :].rearrange("b p k c n -> (b p) k (c n)")

        SPLIT = [(0, HALF, HD ** -0.5), (HALF, 2 * HALF, 1.0), (2 * HALF, 3 * HALF, HD ** -0.5),
                 (3 * HALF, 4 * HALF, 1.0), (4 * HALF, 6 * HALF, 1.0)]
        TG = 2
        NCST = 6

        def by_patches(ap):
            return ap.rearrange("p (r w s) -> p w r s", r=ROWS, s=16)

        def out_bank(m, tail=None):
            return 5 + m if tail is None else 6 + (tail + m) % 2

        block = ctx.enter_context(nc.Block())

        @block.sync
        def _(sp):
            def first_load(c):
                sp.dma_start(first_x[:, c], x_v[0, :, :, c, :]).then_inc(s_first[c], 16)

            sp.dma_start(w_raw[:, :, :], wqkv_t.rearrange("(k p) n -> p k n", p=P)).then_inc(s_raw, 16)
            for c in range(3):
                first_load(c)
            sp.wait_ge(s_split, 1)
            sp.dma_start(w_raw[:, 0, C:3 * C], bqk[0:1, :].to_broadcast([P, 2 * C])).then_inc(s_raw, 16)
            sp.dma_start(w_raw[:, :, 0:C], w_in_t.rearrange("(k p) n -> p k n", p=P)).then_inc(s_raw, 16)
            for dst, src in ((t_mats, mats), (t_gavg, gavg), (t_rowpick, rowpick), (bfc_c, bfc), (wdw, w_dw)):
                sp.dma_start(dst[:], src).then_inc(s_cst, 16)
            sp.wait_ge(s_init, 1)
            sp.dma_start(fsel[0:filt.shape[0], :], filt).then_inc(s_cst, 16)
            for c in range(3, NCH):
                first_load(c)
            for c in range(2):
                sp.dma_start(xa[:, c], x_v[0, :, :, c, :]).then_inc(s_xa[c], 16)
            for dst, src in ((t_csw, cs_w), (t_cosh, cos_h), (t_sinh, sin_h)):
                sp.dma_start(dst[:], src).then_inc(s_tab, 16)
            sp.dma_start(wout[:], w_out_t).then_inc(s_late, 16)
            sp.dma_start(bv_bc[:], bv[0:1, :].to_broadcast([P, C])).then_inc(s_late, 16)
            sp.dma_start(wfc[:], wfc_t.rearrange("(k p) n -> p k n", p=P)).then_inc(s_late, 16)

            def wait(sem, value):
                sp.wait_ge(sem, value)
                sp.sem_inc(s_past, 1)

            with sp.Fori(0, images) as i:
                def load_next(c, h, par):
                    wait(s_stat, i * 8 + c + (NCH - 1))
                    wait(s_st[par], (i * 8 + 1) * 16)
                    sp.dma_start(xr[:, par], chunk_of(x_v, (i + 1) & (images - 1), c)).then_inc(s_xr[par], 16)
                load_next(0, 0, 0)
                load_next(1, 0, 1)

                def load_a(c, h, edge, par):
                    wait(s_lo, (i * 16 + c) * 3 + 9)
                    sp.dma_start(xa[:, par], chunk_of(x_v, i, c + 2)).then_inc(s_xa[par], 16)
                    load_next(c + 2, h + 1, par)
                steps(sp, NCH - 2, 0, NCH - 2, load_a)

                def part_b(c, h, edge, par):
                    if within(edge, 0, NCH, -2):
                        wait(s_res, (i * 16 + c) * 3 + 3)
                        sp.dma_start(chunk_of(x1_v, i, c - 2), xr[:, par]).then_inc(s_st[par], 16)
                    if within(edge, 0, NCH):
                        wait(s_x1s, i * 8 + c + 1)
                        wait(s_st[par], (i * 8 + h + 1) * 16)
                        if edge in (0, 1):
                            wait(s_stat, i * 8 + c + (2 * NCH - 1))
                        sp.dma_start(xr[:, par], chunk_of(x_v, i, c)).then_inc(s_xr[par], 16)
                steps(sp, NCH + 2, 2, NCH, part_b)

                wait(s_x1s, i * 8 + (NCH + 2))

                def load_c(c, h, par):
                    wait(s_lo, (i * 16 + c + NCH) * 3 + 3)
                    wait(s_st[par], (i * 8 + h + 2) * 16)
                    sp.dma_start(xa[:, par], chunk_of(x1_v, i, c)).then_inc(s_xa[par], 16)
                for u in range(2):
                    wait(s_out, (i * 16 + (NCH - 1 + u)) * 3 + 6)
                    load_c(u, 0, u)

                def part_c(c, h, edge, par):
                    if within(edge, 0, NCH, 2):
                        load_c(c + 2, h + 1, par)
                    if edge in (NCH - 2, NCH - 1):
                        wait(s_lo, (i * 16 + c + (NCH + 2)) * 3 + 3)
                        sp.dma_start(xa[:, par], chunk_of(x_v, (i + 1) & (images - 1), c - (NCH - 2)))\
                            .then_inc(s_xa[par], 16)
                    if within(edge, 0, NCH, -2):
                        wait(s_res, (i * 16 + c + NCH) * 3 + 3)
                        sp.dma_start(chunk_of(out_v, i, c - 2), xr[:, par]).then_inc(s_st[par], 16)
                    if within(edge, 0, NCH):
                        wait(s_st[par], (i * 8 + h + 5) * 16)
                        sp.dma_start(xr[:, par], chunk_of(x1_v, i, c)).then_inc(s_xr[par], 16)
                steps(sp, NCH + 2, 2, NCH - 2, part_c)
            for par in range(2):
                wait(s_xa[par], (images * 8 + 1) * 16)
                wait(s_st[par], (images * 8 + 1) * 16)

        @block.gpsimd
        def _(gp):
            nc.gpsimd.memset(fsel[:], 0.0)
            nc.gpsimd.memset(ones_f[:], 1.0)
            nc.gpsimd.memset(vt[:, :, :, P:P + 1], 1.0)
            for j, (s, n) in enumerate(AHEAD.items()):
                nc.gpsimd.memset(counted[:, j:j + 1], 0.0).then_inc(s, n)
            nc.gpsimd.memset(counted[:, len(AHEAD):], 0.0).then_inc(s_init, 1)

            def low_part(m, k, par, patches=False):
                gp.wait_ge(s_hi, m * 3 + (k + 1))
                dst, src, hi = x_lo[:, par, k], xa[:, par, k], x_hi[:, par, k].bitcast(fp32)
                if patches:
                    dst, hi = (ap.rearrange("p (w r s) -> p w r s", r=ROWS, s=16) for ap in (dst, hi))
                    src = by_patches(src)
                nc.gpsimd.tensor_tensor(dst, src, hi, ALU.subtract).then_inc(s_lo, 1)

            def rotated_sum(T, p2):
                gp.wait_ge(s_rope, T + 3)
                a = t1[:, p2].rearrange("p b s (t f) -> p (b s) t f", t=2)
                b = t2[:, p2].rearrange("p b s (t f) -> p (b s) t f", t=2)
                nc.gpsimd.tensor_tensor(a, a, b[:, :, ::-1, :], ALU.add).then_inc(s_add, 1)

            for k in range(KB):
                low_part(0, k, 0)
            with gp.Fori(0, images) as i:
                rotated_sum(i * NT, 0)

                def part_a(c, h, edge, par):
                    T = (i * 8 + c) * 4
                    for j in range(TPC):
                        if j < KB and within(edge, 0, NCH, 1):
                            low_part(i * 16 + c + 1, j, 1 - par)
                        if j < TPC - 1 or within(edge, 0, NCH, 1):
                            rotated_sum(T + j + 1, (j + 1) % 2)
                steps(gp, NCH, 0, NCH - 2, part_a)

                gp.wait_ge(s_ka, i * 5 + 1)
                gp.sem_inc(s_past, 1)

                def times_ksum(c, par):
                    n = i * 8 + c
                    gp.wait_ge(s_tp, n * 3 + 3)
                    nc.gpsimd.tensor_tensor(qn[:, par], q_all[:, ds(c * 4, 4), :],
                                            kbc[:, :].unsqueeze(1).to_broadcast([P, TPC, C]), ALU.mult)\
                        .then_inc(s_prod, 1)

                gp.wait_ge(s_tp, i * NCH * 3 + 3)
                nc.gpsimd.tensor_tensor(qn[:, 0, 0:TG], q_all[:, 0:TG, :],
                                        kbc[:, :].unsqueeze(1).to_broadcast([P, TG, C]), ALU.mult).then_inc(s_prod, 1)

                def part_b(c, h, edge, par):
                    n = i * 8 + c
                    gp.wait_ge(s_nd, n * 3 + 3)
                    gp.sem_inc(s_past, 1)
                    nc.gpsimd.tensor_tensor(qn[:, par, 0:TG].rearrange("p t (h d) -> p (t h) d", d=HD),
                                            q_all[:, ds(c * 4, TG), :].rearrange("p t (h d) -> p (t h) d", d=HD),
                                            nrm[:, 0:TG * HEADS].unsqueeze(2).to_broadcast([P, TG * HEADS, HD]), ALU.mult)\
                        .then_inc(s_qnp, 1)
                    if within(edge, 0, NCH, 1):
                        times_ksum(c + 1, 1 - par)
                steps(gp, NCH, 0, NCH - 2, part_b)

                gp.wait_ge(s_qn, i * NCH + (NCH + 1))
                gp.sem_inc(s_past, 1)
                gp.wait_ge(s_qnp, i * NCH + (NCH + 1))
                gp.sem_inc(s_past, 1)
                nc.gpsimd.memset(filt_img[:, :, 0:HP:HP - 1, :], 0.0)
                nc.gpsimd.memset(filt_img[:, :, 1:HP - 1, 0:WP:WP - 1], 0.0).then_inc(s_brd, 1)
                gp.wait_ge(s_lo, (i * 16 + NCH + 1) * 3 + 6)
                gp.sem_inc(s_past, 1)

                def part_c(c, h, edge, par):
                    for k in range(KB):
                        low_part(i * 16 + c + (NCH + 1), k, 1 - par, patches=True)
                steps(gp, NCH - 1, 0, NCH - 2, part_c)
                for k in range(KB):
                    low_part(i * 16 + 16, k, 0)

        @block.scalar
        def _(act):
            act.wait_ge(s_init, 1)

            def normalise(loads, par):
                act.wait_ge(s_xa[par], loads * 16)
                for k in range(KB):
                    nc.scalar.activation(xa[:, par, k], xa[:, par, k], ACT.Identity, bias=shift[:, 1, k:k + 1],
                                         scale=rstd[:, 1, k:k + 1]).then_inc(s_nrm, 1)

            def high_part(m, par, patches=False):
                act.wait_ge(s_xfree, m + 1)
                for k in range(KB):
                    act.wait_ge(s_nrm, m * 3 + (k + 1))
                    dst, src = x_hi[:, par, k], xa[:, par, k]
                    if patches:
                        dst, src = dst.rearrange("p (w r s) -> p w r s", r=ROWS, s=16), by_patches(src)
                    nc.scalar.activation(dst, src, ACT.Copy).then_inc(s_hi, 1)

            def tile_a(T, p2):
                act.wait_ge(s_add, T + 1)
                nc.scalar.activation(t2[:, p2], t1[:, p2], ACT.Exp).then_inc(s_exp, 1)
                act.wait_ge(s_qkv, T * 3 + 3)
                act.wait_ge(s_kv, T + 1)
                nc.scalar.activation(vt[:, p2, :, 0:P], bank[3 * p2 + 2][:, 0:C].rearrange("p (k n) -> p k n", k=KB),
                                     ACT.Copy).then_inc(s_v, 1)
                act.wait_ge(s_exp, T * 2 + 1)
                nc.scalar.activation(t1[:, p2], t1[:, p2], ACT.Relu).then_inc(s_exp, 1)

            def group_root(f):
                act.wait_ge(s_gs, f * 11 + 5)
                nc.scalar.activation(gstd[:, :, :], gvar[:, :, :], ACT.Sqrt).then_inc(s_ga, 1)

            group_root(0)
            high_part(0, 0)
            with act.Fori(0, images) as i:
                tile_a(i * NT, 0)

                def part_a(c, h, edge, par):
                    T = (i * 8 + c) * 4
                    for j in range(TPC):
                        if j == 0 and within(edge, 0, NCH, 1):
                            high_part(i * 16 + c + 1, 1 - par)
                        if j < TPC - 1 or within(edge, 0, NCH, 1):
                            tile_a(T + j + 1, (j + 1) % 2)
                steps(act, NCH, 0, NCH - 2, part_a)

                act.wait_ge(s_kp, i * 5 + 1)
                nc.scalar.activation(kbc[:, :], bank[0][:, 0:C], ACT.Copy).then_inc(s_ka, 1)
                act.wait_ge(s_kp, i * 5 + 2)
                nc.scalar.activation(kv_t[:, :, :], bank[1][:, 0:C].rearrange("p (k n) -> p k n", k=KB), ACT.Copy)\
                    .then_inc(s_ka, 1)
                for j in range(KB):
                    act.wait_ge(s_kp, i * 5 + 3 + j)
                    nc.scalar.activation(mout_hi[:, j], bank[2 + j][:, 0:C], ACT.Copy).then_inc(s_ka, 1)

                def part_b(c, h, edge, par):
                    n = i * 8 + c
                    act.wait_ge(s_out, (i * 16 + c) * 3 + 3)
                    for j in range(KB):
                        act.wait_ge(s_tp, n * 3 + (j + 7))
                        nc.scalar.activation(qt_hi[:, par, j], bank[(par + j) % 2][:, :], ACT.Copy).then_inc(s_qt, 1)
                steps(act, NCH, 0, NCH, part_b)
                group_root(i + 1)

                def copy_t(T, p2):
                    act.wait_ge(s_tm, T + 1)
                    act.wait_ge(s_dft, T + 1)
                    nc.scalar.activation(tb[:, p2], bank[p2][:, 0:C], ACT.Copy).then_inc(s_t, 1)

                def copy_img(T, c, j):
                    act.wait_ge(s_inv, T + 3)
                    dst = filt_img[:, :, ds(c * ROWS + 1, ROWS), 1 + 16 * j:17 + 16 * j]
                    src = bank[4][:, 0:C].rearrange("p (k r s) -> p k r s", k=KB, s=16)
                    nc.scalar.activation(dst, src, ACT.Copy).then_inc(s_img, 1)

                def gelu(c, m):
                    n = i * 8 + c
                    act.wait_ge(s_dw, n * ND + (ND - 2 + 2 * m))
                    if m == 0:
                        act.wait_ge(s_out, (i * 16 + c) * 3 + 3 * (NCH + 2))
                        nc.scalar.activation(gel[:, 0], acc[:, 0], ACT.Gelu).then_inc(s_gel, 1)
                    else:
                        nc.scalar.activation(gel[HD:P, 1], acc[0:HD, 2], ACT.Gelu).then_inc(s_gel, 1)

                def first_tap(c, k):
                    act.wait_ge(s_img, (i * 8 + c) * 4 + 6)
                    act.wait_ge(s_gate, (i * 8 + c) * 2 + 2)
                    nc.scalar.activation(acc[:, k].rearrange("p (r s) -> p r s", s=W),
                                         filt_img[:, k, ds(c * ROWS, ROWS), 0:W], ACT.Copy, scale=wdw[:, k, 0:1])\
                        .then_inc(s_tap, 1)

                act.wait_ge(s_gs, (i + 1) * 11 + 11)
                act.wait_ge(s_brd, i + 1)
                act.sem_inc(s_past, 1)
                for u in range(2):
                    high_part(i * 16 + (NCH + u), u, patches=True)

                def part_c(c, h, edge, par):
                    T = (i * 8 + c) * 4
                    tile, conv, gated = (within(edge, 0, NCH, -d) for d in range(3))
                    if tile:
                        copy_t(T, 0)
                    if gated:
                        gelu(c - 2, 0)
                        gelu(c - 2, 1)
                    if tile:
                        copy_t(T + 1, 1)
                    if conv and edge != 1:
                        first_tap(c - 1, KB - 1)
                    if tile:
                        copy_t(T + 2, 0)
                        copy_img(T, c, 0)
                        copy_t(T + 3, 1)
                        if within(edge, 0, NCH, 1) and edge != 0:
                            normalise(i * 8 + 5 + h + par, 1 - par)
                        copy_img(T + 1, c, 1)
                        if within(edge, 0, NCH, 1) and edge != 0:
                            high_part(i * 16 + c + (NCH + 1), 1 - par, patches=True)
                        if edge == NCH - 1:
                            high_part(i * 16 + 16, 0)
                        copy_img(T + 2, c, 2)
                        copy_img(T + 3, c, 3)
                    if edge == 0:
                        first_tap(c, KB - 1)
                steps(act, NCH + 2, 2, NCH - 2, part_c)

        @block.vector
        def _(dve):
            dve.wait_ge(s_init, 1)
            nc.vector.tensor_copy(ones_r[:], ones_f[:])
            nc.vector.memset(bn_x1[:], 1.0)
            nc.vector.memset(gvar[:], 1.0)
            dve.wait_ge(s_raw, 16)
            count = [0]

            def link(ins):
                count[0] += 1
                ins.then_inc(s_link, 1)
                dve.wait_ge(s_link, count[0])

            def split(hi, lo, raw, scale):
                link(nc.vector.tensor_scalar(hi, raw, scale, None, ALU.mult))
                return nc.vector.scalar_tensor_tensor(lo, raw, scale, hi.bitcast(fp32), ALU.mult, ALU.subtract)

            for a, b, scale in SPLIT:
                ins = split(w_hi[:, :, a:b], w_lo[:, :, a:b], w_raw[:, :, a:b], scale)
            ins.then_inc(s_split, 1)

            def first_stats(c):
                dve.wait_ge(s_first[c], 16)
                for k in range(KB):
                    ins = nc.vector.bn_stats(bn_x[:, k, c, :], first_x[:, c, k])
                ins.then_inc(s_stat, 1)

            for c in range(3):
                first_stats(c)

            dve.wait_ge(s_raw, 48)
            link(split(win_hi[:], win_lo[:], w_raw[:, :, 0:C], 1.0))
            dve.wait_ge(s_cst, NCST * 16)
            for a, b, scale in SPLIT[:4]:
                hi, raw = qkbias[:, a:b], w_raw[:, 0, C + a:C + b]
                tmp = w_raw[:, 1, C + a:C + b]
                link(split(hi, tmp, raw, scale))
                link(nc.vector.tensor_scalar(tmp, tmp, t_rowpick[:, 1:2], None, ALU.mult))
                ins = nc.vector.scalar_tensor_tensor(hi, hi.bitcast(fp32), t_rowpick[:, 0:1], tmp, ALU.mult, ALU.add)
            ins.then_inc(s_split, 1)
            for c in range(3, NCH):
                first_stats(c)

            def group_norm(f):
                g = f * 11

                def nxt(ins, k):
                    ins.then_inc(s_gs, 1)
                    dve.wait_ge(s_gs, g + k)

                dve.wait_ge(s_stat, f * NCH + NCH)
                dve.wait_ge(s_x1s, f * NCH + 2)
                dve.sem_inc(s_past, 1)
                for s, bn in enumerate((bn_x, bn_x1)):
                    for k in range(KB):
                        ins = nc.vector.bn_aggr(mv[:, s, k], bn[:, k].rearrange("p c s -> p (c s)"))
                nxt(ins, 1)
                dve.wait_ge(s_gp, f * 2 + 1)
                pm = bank[7][:, 0:2 * KB].rearrange("p (m s) -> p s m", s=2)
                nc.vector.tensor_copy(gmean[:, :, :], pm)
                nxt(nc.vector.tensor_tensor(dev[:, :, :], mv[:, :, :, 0], pm, ALU.subtract), 2)
                nxt(nc.vector.tensor_tensor(newt[:, :, :], dev[:, :, :], dev[:, :, :], ALU.mult), 3)
                nxt(nc.vector.tensor_tensor(dev[:, :, :], newt[:, :, :], mv[:, :, :, 1], ALU.add), 4)
                dve.wait_ge(s_gp, f * 2 + 2)
                nxt(nc.vector.tensor_scalar(gvar[:, :, :], pm, GN_EPS, None, ALU.add), 5)
                dve.wait_ge(s_ga, f + 1)
                nxt(nc.vector.reciprocal(rstd[:, :, :], gstd[:, :, :]), 6)
                nxt(nc.vector.tensor_tensor(newt[:, :, :], rstd[:, :, :], rstd[:, :, :], ALU.mult), 7)
                nxt(nc.vector.tensor_tensor(newt[:, :, :], newt[:, :, :], gvar[:, :, :], ALU.mult), 8)
                nxt(nc.vector.tensor_scalar(newt[:, :, :], newt[:, :, :], -0.5, 1.5, ALU.mult, ALU.add), 9)
                nxt(nc.vector.tensor_tensor(rstd[:, :, :], rstd[:, :, :], newt[:, :, :], ALU.mult), 10)
                nxt(nc.vector.scalar_tensor_tensor(shift[:, :, :], gmean[:, :, :], -1.0, rstd[:, :, :], ALU.mult, ALU.mult), 11)

            group_norm(0)

            def convolution_constants():
                for k in range(PE_BLOCKS):
                    for q in range(PE_TAPS):
                        nc.vector.tensor_scalar(tapdiag[:, k, q], ident, wdw[:, k, q:q + 1], None, ALU.mult)
                dve.wait_ge(s_filter, 1)
                nc.vector.tensor_copy(fsel[:], bank[6][:, 0:C]).then_inc(s_split, 1)

            def normalise(s, loads, par):
                dve.wait_ge(s_xa[par], loads * 16)
                for k in range(KB):
                    nc.vector.tensor_scalar(xa[:, par, k], xa[:, par, k], gmean[:, s, k:k + 1],
                                            rstd[:, s, k:k + 1], ALU.subtract, ALU.mult).then_inc(s_nrm, 1)

            def rope(T, tile, p2):
                wide = [P, 2, ROT, 2]
                dve.wait_ge(s_elu, T + 1)
                tabs = [(t_cosh[:, ds(tile, 1), :].rearrange("p a f -> p (a f)"),
                         t_sinh[:, ds(tile, 1), :].rearrange("p a f -> p (a f)")),
                        (t_csw[:, 0, :], t_csw[:, 1, :])]
                for b in range(2):
                    dve.wait_ge(s_qkv, T * 3 + (b + 1))
                    src = bank[3 * p2 + b][:, 0:C].rearrange("p (s f r) -> p s f r", s=2, r=2)
                    for dst, tab in zip((t1, t2), tabs[b]):
                        ins = nc.vector.tensor_tensor(dst[:, p2, b].rearrange("p s (f r) -> p s f r", r=2), src,
                                                      tab.unsqueeze(1).unsqueeze(3).to_broadcast(wide), ALU.mult)
                ins.then_inc(s_rope, 1)

            def elu(T, tile, p2):
                dve.wait_ge(s_exp, T * 2 + 2)
                dve.wait_ge(s_kv, T + 1)
                qdst = q_all[:, ds(tile, 1), :].rearrange("p a (b f) -> p (a b) f", b=2)
                for s, dst in enumerate((qdst, kt[:, p2].rearrange("p (b f) -> p b f", b=2))):
                    ins = nc.vector.scalar_tensor_tensor(dst, t2[:, p2, :, s], 1.0, t1[:, p2, :, s], ALU.min, ALU.add)
                ins.then_inc(s_elu, 1)

            normalise(0, 1, 0)
            convolution_constants()
            dve.wait_ge(s_tab, 48)
            rope(0, 0, 0)
            with dve.Fori(0, images) as i:

                def part_a(c, h, edge, par):
                    T = (i * 8 + c) * 4
                    if within(edge, 0, NCH, 1):
                        normalise(0, i * 8 + 1 + h + par, 1 - par)
                    for j in range(TPC):
                        if j > 0:
                            if j == 1:
                                dve.wait_ge(s_xr[par], (i * 12 + 1 + h) * 16)
                            ins = nc.vector.bn_stats(bn_x[:, j - 1, ds(c, 1), :].rearrange("p c s -> p (c s)"), xr[:, par, j - 1])
                            if j == KB:
                                ins.then_inc(s_stat, 1)
                        if j < TPC - 1 or within(edge, 0, NCH, 1):
                            rope(T + j + 1, c * 4 + (j + 1), (j + 1) % 2)
                        elu(T + j, c * 4 + j, j % 2)
                steps(dve, NCH, 0, NCH - 2, part_a)

                kvp = bank[KVB][:, 0:KB * (P + 1)].rearrange("p (k n) -> p k n", k=KB)
                dve.wait_ge(s_kv, i * NT + (NT + 2))
                nc.vector.tensor_copy(ksum[:, :], kvp[:, :, P]).then_inc(s_kd, 1)
                dve.wait_ge(s_lo, (i * 16 + NCH) * 3 + 6)
                dve.wait_ge(s_kd, i * 5 + 1)
                for j in range(KB):
                    ins = nc.vector.tensor_scalar(kdiag[:, j], ident, ksum[:, j:j + 1], None, ALU.mult)
                ins.then_inc(s_kd, 1)
                dve.wait_ge(s_late, 48)
                for j in range(KB):
                    ins = nc.vector.scalar_tensor_tensor(kvfix[:, j], bv_bc[:, j * P:(j + 1) * P], ksum[:, j:j + 1],
                                                         kvp[:, j, 0:P], ALU.mult, ALU.add)
                ins.then_inc(s_kd, 1)
                dve.wait_ge(s_kd, i * 5 + 3)
                nc.vector.tensor_tensor(kvfix[:, :, :], kvfix[:, :, :], headmask.unsqueeze(1).to_broadcast([P, KB, P]),
                                        ALU.mult).then_inc(s_kd, 1)

                def divide_q(c, par):
                    n = i * 8 + c
                    by_head = qn[:, par].rearrange("p t (h d) -> p (t h) d", d=HD)
                    dve.wait_ge(s_prod, n + 1)
                    dve.wait_ge(s_qn, n + 1)
                    dve.wait_ge(s_qnp, n + 1)
                    nc.vector.tensor_reduce(nrm[:, :], by_head, AX.X, ALU.add).then_inc(s_nd, 1)
                    dve.wait_ge(s_nd, n * 3 + 1)
                    nc.vector.tensor_scalar(nrm[:, :], nrm[:, :], NORM_EPS, None, ALU.add).then_inc(s_nd, 1)
                    dve.wait_ge(s_nd, n * 3 + 2)
                    nc.vector.reciprocal(nrm[:, :], nrm[:, :]).then_inc(s_nd, 1)
                    dve.wait_ge(s_nd, n * 3 + 3)
                    nc.vector.tensor_tensor(by_head[:, TG * HEADS:],
                                            q_all[:, ds(c * 4 + TG, TPC - TG), :].rearrange("p t (h d) -> p (t h) d", d=HD),
                                            nrm[:, TG * HEADS:].unsqueeze(2).to_broadcast([P, (TPC - TG) * HEADS, HD]),
                                            ALU.mult).then_inc(s_qn, 1)

                def low_q(c, par, blocks=range(KB)):
                    for j in blocks:
                        dve.wait_ge(s_qt, (i * 8 + c) * 3 + (j + 1))
                        nc.vector.tensor_tensor(qt_lo[:, par, j], bank[(par + j) % 2][:, :], qt_hi[:, par, j].bitcast(fp32),
                                                ALU.subtract).then_inc(s_ql, 1)

                def residual(r, loads, par, bias, tail=None, blocks=(0, 1, 2)):
                    dve.wait_ge(s_xr[par], loads * 16)
                    for m in blocks:
                        dve.wait_ge(s_out, r * 3 + (m + 7))
                        ps = bank[2 + 3 * par + m if bias else out_bank(m, tail)][:, :]
                        if bias:
                            ins = nc.vector.scalar_tensor_tensor(xr[:, par, m], ps, bfc_c[:, m:m + 1], xr[:, par, m],
                                                                 ALU.add, ALU.add)
                        else:
                            ins = nc.vector.tensor_tensor(xr[:, par, m], ps, xr[:, par, m], ALU.add)
                        ins.then_inc(s_res, 1)

                dve.wait_ge(s_ka, i * 5 + 1)
                dve.wait_ge(s_elu, i * NT + (NT + 2))
                nc.vector.tensor_tensor(qn[:, 0, TG:TPC], q_all[:, TG:TPC, :],
                                        kbc[:, :].unsqueeze(1).to_broadcast([P, TPC - TG, C]), ALU.mult).then_inc(s_kd, 1)
                dve.wait_ge(s_kd, i * 5 + 5)
                divide_q(0, 0)
                for j in range(KB):
                    dve.wait_ge(s_ka, i * 5 + 3 + j)
                    nc.vector.tensor_tensor(mout_lo[:, j], bank[2 + j][:, 0:C], mout_hi[:, j].bitcast(fp32), ALU.subtract)\
                        .then_inc(s_mlo, 1)
                low_q(0, 0)

                def part_b(c, h, edge, par):
                    if within(edge, 0, NCH, 1):
                        divide_q(c + 1, 1 - par)
                    if edge == NCH:
                        for m in range(KB):
                            residual(i * 16 + c - 1, i * 12 + 4 + h + par, 1 - par, True, blocks=(m,))
                            dve.wait_ge(s_res, (i * 16 + c) * 3 + (m + 4))
                            ins = nc.vector.bn_stats(bn_x1[:, m, c - 1, :], xr[:, 1 - par, m])
                        ins.then_inc(s_x1s, 1)
                        return
                    if within(edge, 0, NCH, -1):
                        residual(i * 16 + c - 1, i * 12 + 4 + h + par, 1 - par, True)
                    if within(edge, 0, NCH, 1):
                        low_q(c + 1, 1 - par, (0, 1))
                    if within(edge, 0, NCH, -1):
                        dve.wait_ge(s_res, (i * 16 + c) * 3 + 6)
                        for k in range(KB):
                            ins = nc.vector.bn_stats(bn_x1[:, k, ds(c - 1, 1), :].rearrange("p c s -> p (c s)"),
                                                     xr[:, 1 - par, k])
                        ins.then_inc(s_x1s, 1)
                    if within(edge, 0, NCH, 1):
                        low_q(c + 1, 1 - par, (2,))
                steps(dve, NCH + 1, 1, NCH - 1, part_b)
                group_norm(i + 1)

                def times_filter(T, p2):
                    dve.wait_ge(s_dft, T + 3)
                    dve.wait_ge(s_inv, T + 1)
                    nc.vector.tensor_tensor(gb[:, p2], bank[2 + p2][:, 0:C], fsel[:, :], ALU.mult).then_inc(s_f, 1)

                ORDER = [(dy, dx) for dy in (-1, 0, 1) for dx in (-1, 0, 1)]

                def depthwise(c, s0, s1):
                    n = i * 8 + c
                    for s in range(s0, s1):
                        q, k = DW_STEPS[s]
                        dy, dx = ORDER[q]
                        src = filt_img[:, k, ds(c * ROWS + (1 + dy), ROWS), 1 + dx:1 + dx + W]
                        dst = acc[:, k].rearrange("p (r s) -> p r s", s=W)
                        before = [e for e in range(s) if DW_STEPS[e][1] == k]
                        so_far = dst
                        if before:
                            dve.wait_ge(s_dw, n * ND + (before[-1] + 1))
                        elif k < PE_BLOCKS:
                            so_far = bank[5 + k][:, :].rearrange("p (r s) -> p r s", s=W)
                            dve.wait_ge(s_ptap, n * PE_BLOCKS + (k + 1))
                            dve.wait_ge(s_gate, n * 2 + (k + 1))
                        else:
                            dve.wait_ge(s_tap, n + 1)
                        nc.vector.scalar_tensor_tensor(dst, src, wdw[:, k, q:q + 1], so_far, ALU.mult, ALU.add)\
                            .then_inc(s_dw, 1)

                def gate(c, m):
                    n = i * 8 + c
                    dve.wait_ge(s_dw, n * ND + ND)
                    dve.wait_ge(s_gel, n * 2 + (m + 3))
                    a, b = (0, 1) if m == 0 else (HD, 2)
                    nc.vector.tensor_tensor(gel[a:P, m], gel[a:P, m], acc[a:P, b], ALU.mult).then_inc(s_gate, 1)

                normalise(1, i * 8 + 5, 0)
                for k in range(KB):
                    dve.wait_ge(s_hi, (i * 16 + NCH) * 3 + (k + 1))
                    nc.vector.tensor_tensor(x_lo[:, 0, k].rearrange("p (w r s) -> p w r s", r=ROWS, s=16), by_patches(xa[:, 0, k]),
                                            x_hi[:, 0, k].bitcast(fp32).rearrange("p (w r s) -> p w r s", r=ROWS, s=16),
                                            ALU.subtract).then_inc(s_lo, 1)
                normalise(1, i * 8 + 5, 1)
                dve.wait_ge(s_brd, i + 1)

                def part_c(c, h, edge, par):
                    T = (i * 8 + c) * 4
                    tile, conv = within(edge, 0, NCH), within(edge, 0, NCH, -1)
                    parts = (0, 5, 7, 9, ND - 3 * KB) if edge == 1 else (0, 4, 8, 12, ND - 3 * KB)
                    if tile:
                        times_filter(T, 0)
                    if within(edge, 0, NCH, -2):
                        gate(c - 2, 0)
                        if conv:
                            depthwise(c - 1, 0, 1)
                        gate(c - 2, 1)
                    if edge == NCH - 1:
                        normalise(0, i * 8 + 9, 0)
                    if conv and edge != 1:
                        depthwise(c - 1, parts[0] + (1 if within(edge, 0, NCH, -2) else 0), parts[1])
                    if tile:
                        times_filter(T + 1, 1)
                    if conv:
                        depthwise(c - 1, parts[1], parts[2])
                    if tile:
                        times_filter(T + 2, 0)
                    if conv:
                        depthwise(c - 1, parts[2], parts[3])
                    if tile:
                        times_filter(T + 3, 1)
                    if conv:
                        depthwise(c - 1, parts[3], parts[4])
                    if edge == 0:
                        depthwise(c, 0, 5)
                    if edge == NCH + 1:
                        dve.wait_ge(s_gate, i * 16 + 18)
                        rope((i + 1) * NT, 0, 0)
                    if within(edge, 0, NCH, -2):
                        residual(i * 16 + c + (NCH - 2), i * 12 + 8 + h, par, False, 0 if edge == NCH else 3 if edge == NCH + 1 else None,
                                 (0, 1) if conv else (0, 1, 2))
                    if conv:
                        if tile:
                            dve.wait_ge(s_img, T + 6)
                        depthwise(c - 1, ND - 3 * KB, ND)
                        if within(edge, 0, NCH, -2):
                            residual(i * 16 + c + (NCH - 2), i * 12 + 8 + h, par, False, 0 if edge == NCH else None, (2,))
                steps(dve, NCH + 2, 2, NCH - 2, part_c)

        @block.tensor
        def _(pe):
            pe.wait_ge(s_init, 1)
            pe.wait_ge(s_cst, NCST * 16)
            nc.tensor.matmul(bank[6][:, 0:C], sel, fsel[:, :], start=True, stop=True).then_inc(s_filter, 1)

            def group_avg(f):
                for step, (wait, src) in enumerate(((1, lambda k: mv[:, :, k, 0]), (4, lambda k: dev[:, :, k]))):
                    pe.wait_ge(s_gs, f * 11 + wait)
                    for m in range(KB):
                        ks = [k for k, mm in GBLOCKS if mm == m]
                        for k in ks:
                            ins = nc.tensor.matmul(bank[7][:, 2 * m:2 * m + 2], t_gavg[:, GBLOCKS.index((k, m)), :], src(k),
                                                   start=(k == ks[0]), stop=(k == ks[-1]))
                    ins.then_inc(s_gp, 1)

            group_avg(0)
            pe.wait_ge(s_split, 2)

            def split_product(dst, hi, lo, whi, wlo, m=None, first=True):
                for k in range(KB):
                    if m is not None:
                        pe.wait_ge(s_hi, m * 3 + (k + 1))
                    nc.tensor.matmul(dst, hi(k), whi(k), start=first and k == 0, stop=False)
                    nc.tensor.matmul(dst, hi(k), wlo(k), start=False, stop=False)
                for k in range(KB):
                    if m is not None:
                        pe.wait_ge(s_lo, m * 3 + (k + 7))
                    ins = nc.tensor.matmul(dst, lo(k), whi(k), start=False, stop=(k == KB - 1))
                return ins

            def project(T, m, par, j):
                p2 = j % 2
                pe.wait_ge(s_rope, T + 1)
                pe.wait_ge(s_v, T + 1)
                tok = slice(j * P, (j + 1) * P)
                for b in range(3):
                    dst = bank[3 * p2 + b][:, 0:C]
                    cols = slice(b * C, (b + 1) * C)
                    if b < 2:
                        nc.tensor.matmul(dst, ones_r[:, :], qkbias[:, cols], start=True, stop=False)
                    ins = split_product(dst, lambda k: x_hi[:, par, k, tok], lambda k: x_lo[:, par, k, tok],
                                        lambda k: w_hi[:, k, cols], lambda k: w_lo[:, k, cols],
                                        m if j == 0 and b == 0 else None, first=(b == 2))
                    ins.then_inc(s_qkv, 1)

            def add_kv(T, j, first=False, last=False, frees=False):
                pe.wait_ge(s_elu, T + 3)
                pe.wait_ge(s_v, T + 3)
                p2 = j % 2
                for k in range(KB):
                    ins = nc.tensor.matmul(bank[KVB][:, k * (P + 1):(k + 1) * (P + 1)], kt[:, p2, k * P:(k + 1) * P],
                                           vt[:, p2, k, :], start=(first and k == 0), stop=last, skip_group_check=True)
                    if frees and k == 0:
                        ins.then_inc(s_xfree, 1)
                ins.then_inc(s_kv, 1)

            for j in range(2):
                project(j, 0, 0, j)
            with pe.Fori(0, images) as i:
                pe.wait_ge(s_res, i * 48 + 6)

                def part_a(c, h, edge, par):
                    T = (i * 8 + c) * 4
                    first = edge == 0
                    m = i * 16 + c
                    project(T + 2, m, par, 2)
                    add_kv(T, 0, first=first)
                    project(T + 3, m, par, 3)
                    add_kv(T + 1, 1, frees=True)
                    if within(edge, 0, NCH, 1):
                        project(T + 4, m + 1, 1 - par, 0)
                    add_kv(T + 2, 2)
                    if within(edge, 0, NCH, 1):
                        project(T + 5, m + 1, 1 - par, 1)
                    add_kv(T + 3, 3, last=(edge == NCH - 1))

                steps(pe, NCH, 2, NCH - 2, part_a)

                pe.wait_ge(s_kd, i * 5 + 2)
                nc.tensor.matmul(bank[0][:, 0:C], ones_f[:, :], kdiag[:, :, :], start=True, stop=True).then_inc(s_kp, 1)
                pe.wait_ge(s_kd, i * 5 + 4)
                for j in range(KB):
                    ins = nc.tensor.transpose(bank[1][:, j * P:(j + 1) * P], kvfix[:, j], ident)
                ins.then_inc(s_kp, 1)
                pe.wait_ge(s_ka, i * 5 + 2)
                pe.wait_ge(s_late, 48)
                for j in range(KB):
                    nc.tensor.matmul(bank[2 + j][:, 0:C], kv_t[:, j], wfc[:, j], start=True, stop=True).then_inc(s_kp, 1)

                def transpose_q(c, par, blocks=range(KB)):
                    n = i * 8 + c
                    pe.wait_ge(s_qn, n + 2)
                    pe.wait_ge(s_qnp, n + 2)
                    for j in blocks:
                        pe.wait_ge(s_ql, n * 3 + (j + 1))
                        for u in range(TPC):
                            ins = nc.tensor.transpose(bank[(par + j) % 2][:, u * P:(u + 1) * P],
                                                      qn[:, par, u, j * P:(j + 1) * P], ident)
                        ins.then_inc(s_tp, 1)

                transpose_q(0, 0)
                pe.wait_ge(s_ka, i * 5 + 5)
                pe.wait_ge(s_mlo, i * 3 + 3)
                pe.sem_inc(s_past, 1)

                def part_b(c, h, edge, par):
                    r = (i * 16 + c) * 3
                    for m in range(KB):
                        if m == KB - 1 and within(edge, 0, NCH, 1):
                            transpose_q(c + 1, 1 - par)
                        pe.wait_ge(s_res, r + (m + 1))
                        dst = bank[2 + 3 * par + m][:, :]
                        cols = slice(m * P, (m + 1) * P)
                        for j in range(KB):
                            if m == 0:
                                pe.wait_ge(s_qt, (i * 8 + c) * 3 + (j + 1))
                            nc.tensor.matmul(dst, mout_hi[:, j, cols], qt_hi[:, par, j], start=(j == 0), stop=False)
                            nc.tensor.matmul(dst, mout_lo[:, j, cols], qt_hi[:, par, j], start=False, stop=False)
                        for j in range(KB):
                            if m == 0:
                                pe.wait_ge(s_ql, (i * 8 + c) * 3 + (j + 3))
                            ins = nc.tensor.matmul(dst, mout_hi[:, j, cols], qt_lo[:, par, j], start=False, stop=(j == KB - 1))
                        ins.then_inc(s_out, 1)
                steps(pe, NCH, 0, NCH - 2, part_b)
                group_avg(i + 1)

                pe.wait_ge(s_split, 3)
                pe.wait_ge(s_res, i * 48 + (3 * NCH + 6))

                def t_tile(T, m, par, j):
                    p2 = j % 2
                    pe.wait_ge(s_t, T + 1)
                    pix = slice(j * P, (j + 1) * P)
                    split_product(bank[p2][:, 0:C], lambda k: x_hi[:, par, k, pix], lambda k: x_lo[:, par, k, pix],
                                  lambda k: win_hi[:, k], lambda k: win_lo[:, k], m if j == 0 else None).then_inc(s_tm, 1)

                def dft_tile(T, j):
                    p2 = j % 2
                    pe.wait_ge(s_t, T + 3)
                    pe.wait_ge(s_f, T + 1)
                    nc.tensor.matmul(bank[2 + p2][:, 0:C], phi, tb[:, p2], start=True, stop=True).then_inc(s_dft, 1)

                def inverse_tile(T, j, frees=False):
                    p2 = j % 2
                    pe.wait_ge(s_f, T + 3)
                    pe.wait_ge(s_img, T + 2)
                    for k in range(KB):
                        ins = nc.tensor.matmul(bank[4][:, k * P:(k + 1) * P], gb[:, p2, k * P:(k + 1) * P], phi_t,
                                               start=True, stop=True)
                        if frees and k == 0:
                            ins.then_inc(s_xfree, 1)
                    ins.then_inc(s_inv, 1)

                def out_block(c, m, tail=None):
                    pe.wait_ge(s_gate, (i * 8 + c) * 2 + 4)
                    if tail is None and m < PE_BLOCKS:
                        pe.wait_ge(s_dw, (i * 8 + c + 1) * ND + (m + 1))
                    if tail == 0 and m == 0:
                        pe.wait_ge(s_dw, (i * 8 + c + 1) * ND + 2)
                    pe.wait_ge(s_res, (i * 16 + c + NCH) * 3 + (m + (4 if tail is None else 5)))
                    dst = bank[out_bank(m, tail)][:, :]
                    nc.tensor.matmul(dst, wout[:, 0, m * P:(m + 1) * P], gel[:, 0], start=True, stop=False)
                    nc.tensor.matmul(dst, wout[HD:P, 1, m * P:(m + 1) * P], gel[HD:P, 1], start=False, stop=True)\
                        .then_inc(s_out, 1)

                def taps(c):
                    n = i * 8 + c
                    pe.wait_ge(s_img, n * 4 + 6)
                    for k in range(PE_BLOCKS):
                        pe.wait_ge(s_res, (i * 16 + c + (NCH - 1)) * 3 + (k + 4))
                        for q in range(PE_TAPS):
                            ins = nc.tensor.matmul(bank[5 + k][:, :], tapdiag[:, k, q], filt_img[:, k, ds(c * ROWS, ROWS), q:q + W],
                                                   start=(q == 0), stop=(q == PE_TAPS - 1))
                        ins.then_inc(s_ptap, 1)

                def part_c(c, h, edge, par):
                    T = (i * 8 + c) * 4
                    m = i * 16 + c + NCH
                    tile, prod = within(edge, 0, NCH), within(edge, 0, NCH, -2)
                    tail = None if tile else 3 * (c - NCH)
                    if tile:
                        t_tile(T, m, par, 0)
                        t_tile(T + 1, m, par, 1)
                        dft_tile(T, 0)
                    if within(edge, 0, NCH, -1) and edge != 1:
                        taps(c - 1)
                    if tile:
                        t_tile(T + 2, m, par, 2)
                        dft_tile(T + 1, 1)
                        inverse_tile(T, 0)
                    if edge == NCH:
                        pe.wait_ge(s_res, i * 48 + (3 * (2 * NCH - 2) - 2 + 6))
                        pe.wait_ge(s_img, (i + 1) * NT + 2)
                        pe.wait_ge(s_f, (i + 1) * NT + 2)
                        pe.wait_ge(s_t, (i + 1) * NT + 2)
                        project((i + 1) * NT, (i + 1) * 16, 0, 0)
                    if prod:
                        out_block(c - 2, 0, tail)
                    if tile:
                        t_tile(T + 3, m, par, 3)
                        dft_tile(T + 2, 2)
                        inverse_tile(T + 1, 1, frees=True)
                    if prod:
                        out_block(c - 2, 1, tail)
                    if tile:
                        dft_tile(T + 3, 3)
                        inverse_tile(T + 2, 2)
                        inverse_tile(T + 3, 3)
                    if prod:
                        out_block(c - 2, 2, tail)
                    if edge == 0:
                        taps(c)
                    if edge == NCH:
                        project((i + 1) * NT + 1, (i + 1) * 16, 0, 1)
                steps(pe, NCH + 2, 2, NCH, part_c)


def kernel(x, L0_conv_Wq, L0_conv_bq, L0_conv_Wk, L0_conv_bk, L0_conv_Wv, L0_conv_bv, L0_conv_Wfc, L0_conv_bfc,
           L1_conv_fft_filter, L1_conv_w_in, L1_conv_w_dw, L1_conv_w_out):
    import concourse.bacc as bacc
    from concourse.bass_utils import run_bass_kernel_spmd

    a = np.asarray
    images = x.shape[0]
    wq, wk, wv = a(L0_conv_Wq).T, a(L0_conv_Wk).T, a(L0_conv_Wv).T
    bq, bk = a(L0_conv_bq), a(L0_conv_bk)
    half = C // 2
    order = np.concatenate([np.arange(P), half + np.arange(P), np.arange(P, half), half + np.arange(P, half)])
    wo = a(L1_conv_w_out).T
    wout = np.zeros((P, 2, C), wo.dtype)
    wout[:, 0] = wo[:P]
    wout[HD:, 1] = wo[P:]
    arrays = {
        "x": a(x).reshape(images, C, NTOK),
        "wqkv_t": np.concatenate([wq[:, :HALF], wk[:, :HALF], wq[:, HALF:], wk[:, HALF:], wv], axis=1),
        "bqk": np.concatenate([bq[:HALF], bk[:HALF], bq[HALF:], bk[HALF:]])[None],
        "bv": a(L0_conv_bv)[None],
        "wfc_t": a(L0_conv_Wfc).T,
        "bfc": a(L0_conv_bfc).reshape(KB, P).T,
        "filt": a(L1_conv_fft_filter)[order].reshape(C, -1).T,
        "w_in_t": a(L1_conv_w_in)[order].T,
        "w_dw": a(L1_conv_w_dw)[order].reshape(KB, P, TAPS).transpose(1, 0, 2),
        "w_out_t": wout,
    }
    arrays.update(constants())
    arrays = {k: np.ascontiguousarray(v) for k, v in arrays.items()}
    nc = bacc.Bacc("TRN2", target_bir_lowering=False, num_devices=1)
    aps = {k: nc.dram_tensor(k, v.shape, mybir.dt.from_np(v.dtype), kind="ExternalInput").ap() for k, v in arrays.items()}
    out = nc.dram_tensor("out", (images, C, NTOK), mybir.dt.float32, kind="ExternalOutput").ap()
    build_program(nc, **aps, out=out, images=images)
    r = run_bass_kernel_spmd(nc, [arrays], core_ids=[0])
    return r.results[0]["out"].reshape(images, C, H, W)
```
